# Optimizing a Trainium2 kernel written in Bass

```python
import numpy as np
import jax
import jax.numpy as jnp

def _softmax(x, axis=-1):
    return jax.nn.softmax(x, axis=axis)

def _gelu(x):
    return jax.nn.gelu(x, approximate=True)

def _silu(x):
    return jax.nn.silu(x)

def _sigmoid(x):
    return jax.nn.sigmoid(x)

def _layernorm(x, axis=-1, eps=1e-05):
    m = jnp.mean(x, axis=axis, keepdims=True)
    v = jnp.var(x, axis=axis, keepdims=True)
    return (x - m) / jnp.sqrt(v + eps)

def _scatter_add(tgt, idx, src, axis=0):
    return tgt.at[idx].add(src)

def _segment_sum(src, seg, n):
    return jax.ops.segment_sum(src, seg, n)
kernel_name = 'mk_macaron_d1_jaxref_r8_591c04'

def setup_inputs(seed: int=0):
    np.random.seed(seed)
    _w = jnp.asarray

    def _L0_attn_setup():
        import math
        import jax, jax.numpy as jnp
        import numpy as np
        PI = math.pi
        PHI = (1 + math.sqrt(5)) / 2
        B, T, D, H = (4, 128, 128, 16)
        DH = D // H

        def _chamber_beta_init(n_heads, layer_depth=0.5):
            lo = layer_depth * 0.5
            hi = 0.5 + layer_depth * 0.5
            frac = np.arange(n_heads) / max(n_heads - 1, 1)
            depth = lo + frac * (hi - lo)
            return (0.5 + 0.2 * (1.0 - 2.0 * depth)).astype(np.float32)
        key = jax.random.key(seed)
        ks = jax.random.split(key, 10)
        s = 0.02
        x = jax.random.normal(ks[0], (B, T, D), dtype=jnp.float32)
        Wa = jax.random.normal(ks[1], (D, H), jnp.float32) * s
        ba = jnp.zeros((H,), jnp.float32)
        We = jax.random.normal(ks[2], (D, H), jnp.float32) * s
        be = jnp.zeros((H,), jnp.float32)
        Wi = jax.random.normal(ks[3], (D, D), jnp.float32) * s
        Wo = jax.random.normal(ks[4], (D, D), jnp.float32) * s
        Wv = jax.random.normal(ks[5], (D, D), jnp.float32) * s
        Wout = jax.random.normal(ks[6], (D, D), jnp.float32) * s
        chi = jnp.ones((H,), jnp.float32)
        beta_p = jnp.asarray(_chamber_beta_init(H))
        iv_p = jnp.full((H,), 0.5, jnp.float32)
        ov_p = jnp.full((H,), 0.5, jnp.float32)
        return {'x': x, 'Wa': Wa, 'ba': ba, 'We': We, 'be': be, 'Wi': Wi, 'Wo': Wo, 'Wv': Wv, 'Wout': Wout, 'chi': chi, 'beta_p': beta_p, 'iv_p': iv_p, 'ov_p': ov_p}
    _L0_attn_in = _L0_attn_setup()

    def _L0_ffn_setup():
        import jax, jax.numpy as jnp
        import numpy as np
        B, S, D = (4, 512, 128)
        E, I = (8, 256)
        CAPACITY = 2
        K = max(1, int(S / E * CAPACITY))
        key = jax.random.key(seed)
        k1, k2, k3, k4, k5 = jax.random.split(key, 5)
        x = jax.random.normal(k1, (B, S, D), dtype=jnp.float32)
        gate_w = jax.random.normal(k2, (D, E), dtype=jnp.float32) * 0.006
        Wg = jax.random.normal(k3, (E, D, I), dtype=jnp.float32) * 0.02
        Wu = jax.random.normal(k4, (E, D, I), dtype=jnp.float32) * 0.02
        Wd = jax.random.normal(k5, (E, I, D), dtype=jnp.float32) * 0.02
        return {'x': x, 'gate_w': gate_w, 'Wg': Wg, 'Wu': Wu, 'Wd': Wd}
    _L0_ffn_in = _L0_ffn_setup()
    _d = {'L0_attn_x': _L0_attn_in['x'], 'L0_attn_Wa': _L0_attn_in['Wa'], 'L0_attn_ba': _L0_attn_in['ba'], 'L0_attn_We': _L0_attn_in['We'], 'L0_attn_be': _L0_attn_in['be'], 'L0_attn_Wi': _L0_attn_in['Wi'], 'L0_attn_Wo': _L0_attn_in['Wo'], 'L0_attn_Wv': _L0_attn_in['Wv'], 'L0_attn_Wout': _L0_attn_in['Wout'], 'L0_attn_chi': _L0_attn_in['chi'], 'L0_attn_beta_p': _L0_attn_in['beta_p'], 'L0_attn_iv_p': _L0_attn_in['iv_p'], 'L0_attn_ov_p': _L0_attn_in['ov_p'], 'L0_ffn_gate_w': _L0_ffn_in['gate_w'], 'L0_ffn_Wg': _L0_ffn_in['Wg'], 'L0_ffn_Wu': _L0_ffn_in['Wu'], 'L0_ffn_Wd': _L0_ffn_in['Wd']}
    _x0 = _d['L0_attn_x']
    _d['L0_attn_x'] = jax.random.normal(jax.random.fold_in(jax.random.key(seed), 1), (4, 512, 128), dtype=_x0.dtype)
    del _x0
    return _d

def reference(L0_attn_x, L0_attn_Wa, L0_attn_ba, L0_attn_We, L0_attn_be, L0_attn_Wi, L0_attn_Wo, L0_attn_Wv, L0_attn_Wout, L0_attn_chi, L0_attn_beta_p, L0_attn_iv_p, L0_attn_ov_p, L0_ffn_gate_w, L0_ffn_Wg, L0_ffn_Wu, L0_ffn_Wd):

    def _L0_attn_ref(x, Wa, ba, We, be, Wi, Wo, Wv, Wout, chi, beta_p, iv_p, ov_p):
        import math
        import jax, jax.numpy as jnp
        import numpy as np
        PI = math.pi
        PHI = (1 + math.sqrt(5)) / 2
        B, T, D, H = (4, 128, 128, 16)
        DH = D // H

        def _chamber_beta_init(n_heads, layer_depth=0.5):
            lo = layer_depth * 0.5
            hi = 0.5 + layer_depth * 0.5
            frac = np.arange(n_heads) / max(n_heads - 1, 1)
            depth = lo + frac * (hi - lo)
            return (0.5 + 0.2 * (1.0 - 2.0 * depth)).astype(np.float32)
        Bb, Tt, Dd = x.shape
        Hh = Wa.shape[1]
        dh = Dd // Hh
        scale = math.sqrt(dh)
        aperture = jax.nn.sigmoid(x @ Wa + ba)
        expression = jax.nn.sigmoid(x @ We + be)
        inner = (x @ Wi).reshape(Bb, Tt, Hh, dh).transpose(0, 2, 1, 3)
        outer = (x @ Wo).reshape(Bb, Tt, Hh, dh).transpose(0, 2, 1, 3)
        alignment = jnp.einsum('bhqd,bhkd->bhqk', inner, outer) / scale
        attn_align = jax.nn.softmax(alignment, axis=-1)
        attn = attn_align * aperture.transpose(0, 2, 1)[..., :, None] * expression.transpose(0, 2, 1)[..., None, :]
        attn = attn / (attn.sum(axis=-1, keepdims=True) + 1e-08)
        v = (x @ Wv).reshape(Bb, Tt, Hh, dh).transpose(0, 2, 1, 3)
        converged = jnp.einsum('bhqk,bhkd->bhqd', attn, v)
        beta = jax.nn.sigmoid(beta_p)[None, :, None, None]
        iv = jax.nn.sigmoid(iv_p)[None, :, None, None]
        ov = jax.nn.sigmoid(ov_p)[None, :, None, None]
        angle = PI * beta
        ca, sa = (jnp.cos(angle), jnp.sin(angle))
        x_in = converged * iv
        half = dh // 2
        xr, xi = (x_in[..., :half], x_in[..., half:])
        chambered = jnp.concatenate([xr * ca - xi * sa, xr * sa + xi * ca], axis=-1) * ov
        rotated = chambered * jnp.tanh(chi)[None, :, None, None]
        combined = rotated.transpose(0, 2, 1, 3).reshape(Bb, Tt, Dd)
        return combined @ Wout

    def _L0_ffn_ref(x, gate_w, Wg, Wu, Wd):
        import jax, jax.numpy as jnp
        import numpy as np
        B, S, D = (4, 512, 128)
        E, I = (8, 256)
        CAPACITY = 2
        K = max(1, int(S / E * CAPACITY))
        logits = jnp.einsum('bsd,de->bse', x, gate_w)
        affinity = jax.nn.softmax(logits, axis=-1)
        affinity_T = jnp.transpose(affinity, (0, 2, 1))
        gating, index = jax.lax.top_k(affinity_T, K)
        b_idx = jnp.arange(x.shape[0])[:, None, None]
        x_sel = x[b_idx, index]
        g = jnp.einsum('bekd,edi->beki', x_sel, Wg)
        u = jnp.einsum('bekd,edi->beki', x_sel, Wu)
        h = jax.nn.silu(g) * u
        out = jnp.einsum('beki,eid->bekd', h, Wd)
        contrib = out * gating[..., None]
        x_out = jnp.zeros_like(x).at[b_idx, index].add(contrib)
        return x_out
    x = L0_attn_x
    x = x + 0.5 * _L0_ffn_ref(_layernorm(x, axis=-1), L0_ffn_gate_w, L0_ffn_Wg, L0_ffn_Wu, L0_ffn_Wd)
    x = x + _L0_attn_ref(_layernorm(x, axis=-1), L0_attn_Wa, L0_attn_ba, L0_attn_We, L0_attn_be, L0_attn_Wi, L0_attn_Wo, L0_attn_Wv, L0_attn_Wout, L0_attn_chi, L0_attn_beta_p, L0_attn_iv_p, L0_attn_ov_p)
    x = x + 0.5 * _L0_ffn_ref(_layernorm(x, axis=-1), L0_ffn_gate_w, L0_ffn_Wg, L0_ffn_Wu, L0_ffn_Wd)
    return x

_drawn_inputs = setup_inputs


def setup_inputs(seed=0):
    import zlib

    import numpy as np

    out = dict(_drawn_inputs(seed))
    spreads = {'L0_attn_ba': (0.0, 2.0),
     'L0_attn_be': (0.0, 0.8),
     'L0_attn_chi': (1.0, 0.6),
     'L0_attn_iv_p': (0.5, 0.6),
     'L0_attn_ov_p': (0.5, 0.6)}
    factors = {'L0_attn_Wa': 64.0,
     'L0_attn_We': 8.0,
     'L0_attn_Wi': 8.0,
     'L0_attn_Wo': 8.0,
     'L0_attn_Wv': 8.0,
     'L0_attn_Wout': 8.0,
     'L0_attn_beta_p': 8.0,
     'L0_ffn_gate_w': 8.0,
     'L0_ffn_Wg': 8.0,
     'L0_ffn_Wu': 8.0,
     'L0_ffn_Wd': 8.0}
    for name, (base, spread) in spreads.items():
        noise = np.random.default_rng([zlib.crc32(name.encode()), seed]).standard_normal(out[name].shape)
        drawn = base * np.exp(spread * noise) if base else spread * noise
        out[name] = jnp.asarray(drawn.astype(out[name].dtype))
    for name, factor in factors.items():
        out[name] = (out[name] * factor).astype(out[name].dtype)
    return out
```

```python
import math
from contextlib import ExitStack

import concourse.bass as bass
from concourse import mybir

P = 128
F32 = mybir.dt.float32
F32R = mybir.dt.float32r
F16 = mybir.dt.float16
U32 = mybir.dt.uint32
I32 = mybir.dt.int32
ALU = mybir.AluOpType
ACT = mybir.ActivationFunctionType
AX = mybir.AxisListType

LOWEST = -3.0e38
LN_EPS = 1e-5
SUM_EPS = 1e-8


class Steps:

    def __init__(self, eng, sem, turn=0, per=0):
        self.eng, self.sem, self.before, self.n, self.per = eng, sem, turn * per, 0, per

    def did(self, ins):
        self.n += 1
        ins.then_inc(self.sem, 1)

    def settle(self):
        self.eng.wait_ge(self.sem, self.before + self.n)

    def end_turn(self):
        assert self.n == self.per, (self.n, self.per)


def macaron_block(nc, x_in, Wa, ba, We, be, Wi, Wo, Wv, Wout, chi, beta_p, iv_p, ov_p, gate_w, Wg, Wu, Wd, out):
    B, S, D = x_in.shape
    H = Wa.shape[1]
    DH = D // H
    E, _, I = Wg.shape
    K = max(1, int(S / E * 2))
    C = S // P
    T = B * C
    BE = B * E
    MI = I // P
    G = 4
    HG = H // G
    PAIRS = HG // 2
    VW = 32
    SCORE_SCALE = 1.0 / math.sqrt(DH)
    assert D == P and K == P and S == 512 and DH == 8 and H == 16 and MI == 2 and E == 8 and BE == 32

    with ExitStack() as ctx:
        def sb(name, shape, dt=F32):
            return ctx.enter_context(nc.sbuf_tensor(name, shape, dt))

        def sem(name):
            return ctx.enter_context(nc.semaphore(name))

        ident = sb("ident", [P, P])
        zeros = sb("zeros", [P, S], F16)
        token_of_partition = sb("token_of_partition", [P, C])
        token_row = sb("token_row", [P, S])
        row_select = sb("row_select", [BE, BE, P], F16)
        gate_sb = sb("gate_sb", [P, E])
        wi_sb = sb("wi_sb", [P, D])
        wo_sb = sb("wo_sb", [P, D])
        wvae_sb = sb("wvae_sb", [P, D + 2 * H])
        bias_row = sb("bias_row", [P, D + 2 * H])
        wout_sb = sb("wout_sb", [P, D])
        swap_rows = sb("swap_rows", [P, P])
        head_params = sb("head_params", [P, 4])
        wg_sb = sb("wg_sb", [P, 2, I])
        wu_sb = sb("wu_sb", [P, 2, I])
        wd_sb = sb("wd_sb", [P, 2, MI, D])
        x = sb("x", [P, T, D])
        xn = sb("xn", [P, T, D])
        xn_hi = sb("xn_hi", [P, T, D], F16)
        xn_lo = sb("xn_lo", [P, T, D], F16)
        xnT = sb("xnT", [P, B, S])
        stats = sb("stats", [P, T, 6])
        mean_var = sb("mean_var", [P, T, 2])
        std = sb("std", [P, T])
        rstd = sb("rstd", [P, T])
        top = sb("top", [P, T])
        shifted = sb("shifted", [P, C, B, E])
        expo = sb("expo", [P, C, B, E])
        total = sb("total", [P, T])
        rtotal = sb("rtotal", [P, T])
        affinity = sb("affinity", [P, C, B, E])
        values = sb("values", [BE, K])
        index_u = sb("index_u", [BE, K], U32)
        index_f = sb("index_f", [BE, K])
        index_h = sb("index_h", [BE, K], F16)
        gateT = sb("gateT", [P, B, E])
        indexT = sb("indexT", [P, B, E])
        hidden = sb("hidden", [P, 2, MI, B * K])
        index_all = hidden[:].rearrange("p u m s -> p (u m s)").bitcast(F16).rearrange("p (r s) -> p r s", r=BE)
        weighted = sb("weighted", [P, B, D])
        part_hi = sb("part_hi", [P, 2, 2, S], F32R)
        part_lo = sb("part_lo", [P, 2, 2, S], F32R)
        vae_and_gates = sb("vae_and_gates", [P, E * B * K])
        v_end, g_end = T * (D + 2 * H), T * (D + 4 * H)
        vae = vae_and_gates[:, 0:v_end].rearrange("p (t f) -> p t f", t=T)
        gate_exp = vae_and_gates[:, v_end:g_end].rearrange("p (t f) -> p t f", t=T)
        gate_one = vae_and_gates[:, g_end:g_end + T * 2 * H].rearrange("p (t f) -> p t f", t=T)
        expression = sb("expression", [P, T, H])
        z_weight = sb("z_weight", [P, T, H])
        q_stack = sb("q_stack", [P, G, PAIRS, S], F32R)
        k_stack = sb("k_stack", [P, G, HG, S], F32R)
        v_ext = sb("v_ext", [P, G, C, HG, VW])
        neg_max = sb("neg_max", [P, G, C, HG])
        max_rows = sb("max_rows", [HG, 2, S], F32R)
        probs = sb("probs", [P, 8, 2, S])
        pick = probs[:].rearrange("p k c s -> p (k c s)").bitcast(F16).rearrange("p (b c e s) -> p b c e s", b=B, c=C, e=E)
        heads_out = sb("heads_out", [P, 2, S])
        work = heads_out[0:BE]
        den_a = sb("den_a", [P, C, HG])
        den_b = sb("den_b", [P, C, HG])
        den_r = sb("den_r", [P, C, HG])
        combined = sb("combined", [P, T, D])
        combinedT = xnT
        picked = vae_and_gates[:].rearrange("p (e b s) -> p e b s", e=E, b=B)
        silu = heads_out
        wy_hi = part_hi[:].rearrange("p u q (b d) -> p u (q b) d", d=D)[:, :, 0:B]
        wy_lo = part_hi[:].rearrange("p u q (b d) -> p u (q b) d", d=D)[:, :, B:2 * B]
        place = q_stack[:].rearrange("p (u b) q s -> p u (b q) s", u=2)
        moeT = combined[:].rearrange("p (b c) d -> p b (c d)", b=B)
        w_rot = sb("w_rot", [P, D])
        hp = sb("hp", [P, 16])
        row_i = sb("row_i", [P, 2], I32)
        parts_dram = nc.dram_tensor("parts_dram", [2, B, H, 4 * DH, S], F32, kind="Internal").ap()
        zero_rows_dram = nc.dram_tensor("zero_rows_dram", [PAIRS, S], F32, kind="Internal").ap()

        ps = ctx.enter_context(nc.psum_tensor("ps", [P, 8, 512], F32))

        consts_made = sem("consts_made")
        pool_consts = sem("pool_consts")
        x_loaded = [sem(f"x_loaded{b}") for b in range(B)]
        gate_loaded = sem("gate_loaded")
        attn_weights_loaded = sem("attn_weights_loaded")
        zero_rows_stored = sem("zero_rows_stored")
        out_stored = sem("out_stored")

        def by(n, name):
            return [sem(f"{name}{i}") for i in range(n)]

        dve_norm, var_ready, std_ready = by(3, "dve_norm"), by(3, "var_ready"), by(3, "std_ready")
        xn_ready, xn_turned, xnT_ready = by(3, "xn_ready"), by(3, "xn_turned"), by(3, "xnT_ready")
        pool_halves, halves_ready = by(2, "pool_halves"), by(2, "halves_ready")
        logits_ready, dve_route, shifted_ready = by(2, "logits_ready"), by(2, "dve_route"), by(2, "shifted_ready")
        exp_ready, affinity_ready, affinity_turned = by(2, "exp_ready"), by(2, "affinity_ready"), by(2, "affinity_turned")
        topk_ready, topk_turned, topkT_ready = by(2, "topk_ready"), by(2, "topk_turned"), by(2, "topkT_ready")
        index_spread, index_all_ready = by(2, "index_spread"), by(2, "index_all_ready")
        pick_ready, gathered, picked_ready = by(2, "pick_ready"), by(2, "gathered"), by(2, "picked_ready")
        expert_loaded = [by(2, f"expert_loaded{l}_") for l in range(2)]
        gate_up_done, silu_ready = by(2, "gate_up_done"), by(2, "silu_ready")
        hidden_ready = by(2, "hidden_ready")
        down_done = by(2, "down_done")
        weighted_ready = by(2, "weighted_ready")
        scatter_ready = by(2, "scatter_ready")
        scatter_done = by(2, "scatter_done")
        scattered, moeT_ready = by(2, "scattered"), by(2, "moeT_ready")
        moe_turned, x_added = by(2, "moe_turned"), by(2, "x_added")
        qk_projected, qk_hi_ready, qk_lo_ready = sem("qk_projected"), sem("qk_hi_ready"), sem("qk_lo_ready")
        hi_stored, lo_stored = ([by(2, f"{name}_stored{u}_") for u in range(2)] for name in ("hi", "lo"))
        vae_projected, vae_ready = sem("vae_projected"), sem("vae_ready")
        gate_exp_ready, gate_one_ready, gates_ready = sem("gate_exp_ready"), sem("gate_one_ready"), sem("gates_ready")
        swap_ready, wout_swapped, dve_rot, act_rot, rot_ready = (
            sem("swap_ready"), sem("wout_swapped"), sem("dve_rot"), sem("act_rot"), sem("rot_ready"))
        stacks_loaded, max_rows_loaded = by(G, "stacks_loaded"), by(G, "max_rows_loaded")
        max_scores_ready = sem("max_scores_ready")
        max_taken = sem("max_taken")
        max_turned, max_rows_ready = sem("max_turned"), sem("max_rows_ready")
        scores_ready = sem("scores_ready")
        probs_ready = sem("probs_ready")
        probs_used = sem("probs_used")
        values_ready = sem("values_ready")
        heads_copied = sem("heads_copied")
        heads_turned = sem("heads_turned")
        dve_heads = sem("dve_heads")
        heads_normed = sem("heads_normed")
        combined_turned, combinedT_ready = sem("combined_turned"), sem("combinedT_ready")
        attention_out, x_attended = sem("attention_out"), sem("x_attended")
        head_starts = [(hidden_ready[l], MI) for l in range(2)] + [(weighted_ready[l], 1) for l in range(2)] + [
            (scatter_done[l], 2) for l in range(2)] + [
            (max_taken, 2), (scores_ready, 1), (probs_ready, 2), (probs_used, 2), (heads_copied, 1),
            (heads_turned, 2), (heads_normed, 1)]

        MAX_UNITS = HG * C
        EXP_UNITS = HG * 2
        MAX_AFTER = (1, 2, 2, 2, 2, 2, 2, 3)

        block = ctx.enter_context(nc.Block())

        @block.sync
        def _(sp):
            for b in range(B):
                sp.dma_start(x[:, b * C:(b + 1) * C, :], x_in[b].rearrange("(c p) d -> p c d", p=P)).then_inc(x_loaded[b], 16)
            sp.dma_start(gate_sb[:], gate_w).then_inc(gate_loaded, 16)

            def load_expert(l, e, u):
                sp.dma_start(wg_sb[:, u:u + 1, :], Wg.rearrange("e d i -> d e i")[:, bass.ds(e, 1), :]).then_inc(expert_loaded[l][u], 16)
                sp.dma_start(wu_sb[:, u:u + 1, :], Wu.rearrange("e d i -> d e i")[:, bass.ds(e, 1), :]).then_inc(expert_loaded[l][u], 16)
                sp.dma_start(wd_sb[:, u:u + 1], Wd.rearrange("e (m p) d -> p e m d", p=P)[:, bass.ds(e, 1)]).then_inc(expert_loaded[l][u], 16)

            load_expert(0, 0, 0)
            load_expert(0, 1, 1)
            for dst, src in ((wi_sb[:], Wi), (wo_sb[:], Wo), (wvae_sb[:, 0:D], Wv), (wvae_sb[:, D:D + H], Wa),
                             (wvae_sb[:, D + H:], We), (wout_sb[:], Wout),
                             (bias_row[:, D:D + H], ba.rearrange("(a h) -> a h", a=1).broadcast_to([P, H])),
                             (bias_row[:, D + H:], be.rearrange("(a h) -> a h", a=1).broadcast_to([P, H]))):
                sp.dma_start(dst, src).then_inc(attn_weights_loaded, 16)
            for n, param in enumerate((beta_p, iv_p, ov_p, chi)):
                each_row = param.rearrange("(h r a) -> h r a", r=1, a=1).broadcast_to([H, DH, 1])
                sp.dma_start(head_params[:, n:n + 1], each_row).then_inc(attn_weights_loaded, 16)

            def load_experts(l):
                with sp.Fori(1, E // 2) as i:
                    for u in range(2):
                        sp.wait_ge(down_done[l], 2 * i + (u - 1))
                        load_expert(l, 2 * i + u, u)

            load_experts(0)
            sp.wait_ge(consts_made, 10)
            sp.dma_start(zero_rows_dram, zeros[0:PAIRS].bitcast(F32).rearrange("p (a t) -> p a t", a=1).broadcast_to([PAIRS, 2, S // 2])).then_inc(zero_rows_stored, 16)

            for b in range(B):
                for qk in range(2):
                    sp.wait_ge(qk_hi_ready, 2 * b + qk + 1)
                    for part in ((0, 1), (0, 2))[qk]:
                        sp.dma_start(parts_dram[qk, b, :, part * DH:(part + 1) * DH], part_hi[:, b % 2, qk, :].bitcast(F32)).then_inc(hi_stored[b % 2][qk], 16)
                    sp.wait_ge(qk_lo_ready, 2 * b + qk + 1)
                    for part in ((2, 3), (1, 3))[qk]:
                        sp.dma_start(parts_dram[qk, b, :, part * DH:(part + 1) * DH], part_lo[:, b % 2, qk, :].bitcast(F32)).then_inc(lo_stored[b % 2][qk], 16)

            def load_stacks(b, g):
                for qk in range(2):
                    rows = parts_dram[qk].rearrange("b (g pp jj) r t -> g jj b r pp t", g=G, pp=PAIRS)
                    for jj in range(2):
                        at = slice(64 * jj, 64 * jj + 4 * DH)
                        stack = q_stack[at, g] if qk == 0 else k_stack[at, g].rearrange("r (pp jj) t -> r jj pp t", jj=2)[:, jj]
                        sp.dma_start(stack.bitcast(F32), rows[g, jj, bass.ds(b, 1)].squeeze(0)).then_inc(stacks_loaded[g], 16)
                for jj in range(2):
                    sp.dma_start(q_stack[64 * jj + 4 * DH:64 * jj + 4 * DH + 1, g].bitcast(F32), zero_rows_dram).then_inc(stacks_loaded[g], 16)

            def load_max_rows(n, g):
                sp.wait_ge(max_rows_ready, n + 1)
                for jj in range(2):
                    sp.dma_start(q_stack[64 * jj + 32:64 * jj + 33, g].bitcast(F32),
                                 max_rows[2 * jj:2 * jj + 2, g % 2, :].bitcast(F32)).then_inc(max_rows_loaded[g], 16)

            for qk in range(2):
                for u in range(2):
                    sp.wait_ge(hi_stored[u][qk], 32 * B // 2)
                    sp.wait_ge(lo_stored[u][qk], 32 * B // 2)
            sp.wait_ge(zero_rows_stored, 16)
            for g in range(3):
                load_stacks(0, g)
            load_max_rows(0, 0)

            def group_loads(b, g, stacks, rows):
                n = b * G + g
                if stacks:
                    sp.wait_ge(scores_ready, n * EXP_UNITS + 1)
                    load_stacks(b if g == 0 else b + 1, (g + 3) % G)
                if rows:
                    load_max_rows(n + 1, (g + 1) % G)

            with sp.Fori(0, B - 1) as b:
                for g in range(G):
                    group_loads(b, g, True, True)
            for g in range(G):
                group_loads(B - 1, g, g == 0, g < G - 1)

            sp.wait_ge(down_done[0], E)
            load_expert(1, 0, 0)
            load_expert(1, 1, 1)
            load_experts(1)
            for b in range(B):
                sp.wait_ge(x_added[1], b + 1)
                sp.dma_start(out[b].rearrange("(c p) d -> p c d", p=P), x[:, b * C:(b + 1) * C, :]).then_inc(out_stored, 16)
            sp.wait_ge(out_stored, 16 * B)

        @block.gpsimd
        def _(pool):
            for counter, start in head_starts:
                pool.sem_inc(counter, start)
            nc.gpsimd.memset(ident[:], 0.0).then_inc(pool_consts, 1)
            nc.gpsimd.memset(row_select[:], 0.0).then_inc(pool_consts, 1)
            nc.gpsimd.memset(v_ext[:], 0.0).then_inc(pool_consts, 1)
            pool.wait_ge(pool_consts, 3)
            nc.gpsimd.affine_select(out=ident[:], in_=ident[:], compare_op=ALU.not_equal, fill=1.0, base=0,
                                    pattern=[[-1, P]], channel_multiplier=1).then_inc(consts_made, 1)
            nc.gpsimd.affine_select(out=row_select[:], in_=row_select[:], compare_op=ALU.not_equal, fill=1.0, base=0,
                                    pattern=[[-1, BE], [0, P]], channel_multiplier=1).then_inc(consts_made, 1)
            nc.gpsimd.iota(token_of_partition[:], pattern=[[P, C]], base=0, channel_multiplier=1,
                           allow_small_or_imprecise_dtypes=True).then_inc(consts_made, 1)
            nc.gpsimd.iota(token_row[:], pattern=[[1, S]], base=0, channel_multiplier=0,
                           allow_small_or_imprecise_dtypes=True).then_inc(consts_made, 1)
            nc.gpsimd.iota(row_i[:, 0:1], pattern=[[0, 1]], base=0, channel_multiplier=1).then_inc(consts_made, 1)
            nc.gpsimd.memset(zeros[:], 0.0).then_inc(consts_made, 1)
            nc.gpsimd.memset(bias_row[:, 0:D], 0.0).then_inc(consts_made, 1)
            pool.wait_ge(consts_made, 7)
            nc.gpsimd.memset(k_stack[:].bitcast(F32), 0.0).then_inc(pool_consts, 1)
            pool.wait_ge(pool_consts, 4)
            for jj in range(2):
                ones_rows = k_stack[64 * jj + 4 * DH:64 * jj + 4 * DH + 1].rearrange("r g (pp jj) t -> r g jj pp t", jj=2)[:, :, jj]
                nc.gpsimd.memset(ones_rows.bitcast(F32), 1.0).then_inc(consts_made, 1)
                pool.wait_ge(consts_made, 8 + jj)
            nc.gpsimd.memset(v_ext[:, :, :, :, DH + 1:DH + 2], 1.0).then_inc(consts_made, 1)

            def halves(l):
                for b in range(B):
                    t = slice(b * C, (b + 1) * C)
                    pool.wait_ge(xn_ready[2 * l], C * (b + 1))
                    nc.gpsimd.tensor_copy(xn_hi[:, t], xn[:, t]).then_inc(pool_halves[l], 1)
                    pool.wait_ge(pool_halves[l], b + 1)
                    nc.gpsimd.tensor_tensor(xn_lo[:, t], xn[:, t], xn_hi[:, t], ALU.subtract).then_inc(halves_ready[l], 1)

            halves(0)
            pool.wait_ge(gates_ready, 2)

            def extend_values(b):
                for g in range(G):
                    if not isinstance(b, int):
                        pool.wait_ge(probs_used, b * (2 * G) + (2 * (g - G) + 4))
                    heads = slice(g * HG, (g + 1) * HG)
                    ex = expression[:, bass.ds(b * C, C), heads].unsqueeze(3)
                    v = vae[:, bass.ds(b * C, C), g * HG * DH:(g + 1) * HG * DH].rearrange("p c (j d) -> p c j d", d=DH)
                    nc.gpsimd.tensor_tensor(v_ext[:, g, :, :, 0:DH], v, ex.broadcast_to([P, C, HG, DH]), ALU.mult).then_inc(values_ready, 1)
                    nc.gpsimd.tensor_copy(v_ext[:, g, :, :, DH:DH + 1], ex).then_inc(values_ready, 1)

            extend_values(0)
            with pool.Fori(1, B) as b:
                extend_values(b)
            halves(1)

        @block.scalar
        def _(act):
            def roots(n):
                for b in range(B):
                    t = slice(b * C, (b + 1) * C)
                    act.wait_ge(var_ready[n], b + 1)
                    nc.scalar.activation(std[:, t], mean_var[:, t, 1], ACT.Sqrt).then_inc(std_ready[n], 1)

            def copy_xnT(n, b):
                act.wait_ge(xn_turned[n], b + 1)
                nc.scalar.copy(xnT[:, b, :], ps[:, b, :]).then_inc(xnT_ready[n], 1)

            def rotation():
                act.wait_ge(attn_weights_loaded, 16 * 12)
                nc.scalar.activation(hp[:, 0:3], head_params[:, 0:3], ACT.Exp, scale=-1.0).then_inc(act_rot, 1)
                nc.scalar.activation(hp[:, 3:4], head_params[:, 3:4], ACT.Tanh).then_inc(act_rot, 1)
                act.wait_ge(rot_ready, 1)
                nc.scalar.activation(hp[:, 10:12], hp[:, 8:10], ACT.Sin).then_inc(act_rot, 1)

            def route(l):
                roots(2 * l)
                for b in range(B):
                    copy_xnT(2 * l, b)
                act.wait_ge(shifted_ready[l], 1)
                nc.scalar.activation(expo[:], shifted[:], ACT.Exp).then_inc(exp_ready[l], 1)
                if l == 0:
                    rotation()
                act.wait_ge(topk_turned[l], 1)
                nc.scalar.copy(gateT[:].rearrange("p b e -> p (b e)"), ps[:, 6, 0:BE]).then_inc(topkT_ready[l], 1)
                nc.scalar.copy(indexT[:].rearrange("p b e -> p (b e)"), ps[:, 6, BE:2 * BE]).then_inc(topkT_ready[l], 1)
                for b in range(B):
                    act.wait_ge(index_spread[l], b + 1)
                    banks = slice(2 * (b % 2), 2 * (b % 2) + 2)
                    nc.scalar.copy(index_all[:, b * E:(b + 1) * E, :].rearrange("p e s -> p (e s)"),
                                   ps[:, banks, :].rearrange("p a s -> p (a s)")).then_inc(index_all_ready[l], 1)
                for n in range(2 * B):
                    b, first = n // 2, 4 * (n % 2)
                    act.wait_ge(gathered[l], n + 1)
                    nc.scalar.copy(picked[:, first:first + 4, b, :],
                                   ps[:, 4 + n % 4, :].rearrange("p (e s) -> p e s", e=4)).then_inc(picked_ready[l], 1)

            def experts(l):
                with act.Fori(0, E // 2) as i:
                    for u in range(2):
                        for m in range(MI):
                            act.wait_ge(gate_up_done[l], i * (4 * MI) + (2 * MI * u + 2 * m + 1))
                            act.wait_ge(hidden_ready[l], i * (2 * MI) + (MI * u + m + 1))
                            nc.scalar.activation(silu[:, m, :], ps[:, 4 + 2 * m, :], ACT.Silu).then_inc(silu_ready[l], 1)
                for b in range(B):
                    act.wait_ge(scattered[l], b + 1)
                    nc.scalar.mul(moeT[:, b, :], ps[:, b, :], 0.5).then_inc(moeT_ready[l], 1)

            route(0)
            experts(0)
            roots(1)
            for b in range(B):
                copy_xnT(1, b)
                for qk in range(2):
                    act.wait_ge(qk_projected, 2 * b + qk + 1)
                    if b >= 2:
                        act.wait_ge(hi_stored[b % 2][qk], 32 * (b // 2))
                    nc.scalar.copy(part_hi[:, b % 2, qk, :], ps[:, 4 + qk, :]).then_inc(qk_hi_ready, 1)
            act.wait_ge(vae_ready, T // 2)
            nc.scalar.activation(gate_exp, vae[:, :, D:], ACT.Exp, scale=-1.0).then_inc(gate_exp_ready, 1)

            def copy_max_rows(n, slot):
                act.wait_ge(max_turned, n + 1)
                nc.scalar.copy(max_rows[:, slot, :], ps[0:HG, 7, :]).then_inc(max_rows_ready, 1)

            copy_max_rows(0, 0)

            def attend(b, g, has_next):
                n = b * G + g
                for k in range(EXP_UNITS):
                    banks = slice(2 + 2 * (k % 2), 4 + 2 * (k % 2))
                    act.wait_ge(scores_ready, n * EXP_UNITS + (k + 2))
                    act.wait_ge(probs_used, n * 2 + (k // 4 + 1))
                    nc.scalar.activation(probs[:, k].rearrange("p c s -> p (c s)"), ps[:, banks, :].rearrange("p c s -> p (c s)"),
                                         ACT.Exp, scale=SCORE_SCALE).then_inc(probs_ready, 1)
                    if k == 1 and has_next:
                        copy_max_rows(n + 1, (g + 1) % 2)
                act.wait_ge(probs_used, n * 2 + 4)
                act.wait_ge(heads_turned, n + 1)
                nc.scalar.copy(heads_out[:, g % 2, :], ps[:, 6, :]).then_inc(heads_copied, 1)

            with act.Fori(0, B - 1) as b:
                for g in range(G):
                    attend(b, g, True)
            for g in range(G):
                attend(B - 1, g, g < G - 1)
            for b in range(B):
                act.wait_ge(combined_turned, b + 1)
                nc.scalar.copy(combinedT[:, b, :], ps[:, b, :]).then_inc(combinedT_ready, 1)

            route(1)
            experts(1)

        @block.vector
        def _(dve):
            def norm_stats(n, b, steps):
                tiles = range(b * C, (b + 1) * C)
                for t in tiles:
                    steps.did(nc.vector.bn_stats(out=stats[:, t, :], in_=x[:, t, :]))
                steps.settle()
                for t in tiles:
                    steps.did(nc.vector.bn_aggr(out=mean_var[:, t, :], in_=stats[:, t, :]))
                steps.settle()
                v = mean_var[:, b * C:(b + 1) * C, 1]
                nc.vector.tensor_scalar(v, v, LN_EPS, None, ALU.add).then_inc(var_ready[n], 1)

            def norm_apply(n, b, steps):
                t0 = slice(b * C, (b + 1) * C)
                dve.wait_ge(std_ready[n], b + 1)
                steps.did(nc.vector.reciprocal(rstd[:, t0], std[:, t0]))
                steps.settle()
                for t in range(b * C, (b + 1) * C):
                    nc.vector.tensor_scalar(xn[:, t, :], x[:, t, :], mean_var[:, t, 0:1], rstd[:, t:t + 1],
                                            ALU.subtract, ALU.mult).then_inc(xn_ready[n], 1)

            def rotation_angles(steps):
                dve.wait_ge(consts_made, 10)
                swapped = swap_rows[:].rearrange("p (h s q) -> p h s q", s=2, q=DH // 2)
                straight = ident[:].rearrange("p (h s q) -> p h s q", s=2, q=DH // 2)
                for s in range(2):
                    nc.vector.tensor_copy(swapped[:, :, s], straight[:, :, 1 - s]).then_inc(swap_ready, 1)
                steps.did(nc.vector.tensor_scalar(row_i[:, 1:2], row_i[:, 0:1], 4, None, ALU.bitwise_and))
                dve.wait_ge(act_rot, 2)
                steps.did(nc.vector.tensor_scalar(hp[:, 0:3], hp[:, 0:3], 1.0, None, ALU.add))
                steps.settle()
                steps.did(nc.vector.tensor_scalar(hp[:, 15:16], row_i[:, 1:2], -0.5, 1.0, ALU.mult, ALU.add))
                steps.did(nc.vector.reciprocal(hp[:, 4:7], hp[:, 0:3]))
                steps.settle()
                steps.did(nc.vector.tensor_scalar(hp[:, 8:9], hp[:, 4:5], -math.pi, math.pi / 2, ALU.mult, ALU.add))
                steps.settle()
                steps.did(nc.vector.scalar_tensor_tensor(out=hp[:, 7:8], in0=hp[:, 8:9], scalar=-1.0, in1=hp[:, 8:9],
                                                         op0=ALU.mult, op1=ALU.min))
                steps.settle()
                nc.vector.tensor_scalar(hp[:, 9:10], hp[:, 7:8], math.pi / 2, None, ALU.add).then_inc(rot_ready, 1)

            def rotation_rows(steps):
                steps.did(nc.vector.tensor_tensor(hp[:, 12:13], hp[:, 5:6], hp[:, 6:7], ALU.mult))
                steps.settle()
                steps.did(nc.vector.tensor_tensor(hp[:, 12:13], hp[:, 12:13], hp[:, 3:4], ALU.mult))
                steps.settle()
                dve.wait_ge(act_rot, 3)
                steps.did(nc.vector.tensor_tensor(hp[:, 13:14], hp[:, 12:13], hp[:, 10:11], ALU.mult))
                steps.did(nc.vector.tensor_tensor(hp[:, 14:15], hp[:, 12:13], hp[:, 11:12], ALU.mult))
                steps.settle()
                steps.did(nc.vector.tensor_tensor(hp[:, 14:15], hp[:, 14:15], hp[:, 15:16], ALU.mult))
                steps.did(nc.vector.tensor_scalar(w_rot[:], wout_sb[:], hp[:, 13:14], None, ALU.mult))
                steps.settle()
                dve.wait_ge(wout_swapped, 1)
                nc.vector.scalar_tensor_tensor(out=w_rot[:], in0=ps[:, 7, 0:D], scalar=hp[:, 14:15], in1=w_rot[:],
                                               op0=ALU.mult, op1=ALU.add).then_inc(rot_ready, 1)

            def route(l, norm_steps):
                for b in range(B):
                    norm_apply(2 * l, b, norm_steps)
                steps = Steps(dve, dve_route[l])
                logits = ps[:, 4, 0:T * E].rearrange("p (t e) -> p t e", e=E)
                sh, ex, af = (a[:].rearrange("p c b e -> p (c b) e") for a in (shifted, expo, affinity))
                dve.wait_ge(logits_ready[l], 1)
                steps.did(nc.vector.tensor_reduce(top[:], logits, AX.X, ALU.max))
                steps.settle()
                nc.vector.tensor_tensor(sh, logits, top[:].unsqueeze(2).broadcast_to([P, T, E]), ALU.subtract).then_inc(shifted_ready[l], 1)
                dve.wait_ge(exp_ready[l], 1)
                steps.did(nc.vector.tensor_reduce(total[:], ex, AX.X, ALU.add))
                steps.settle()
                steps.did(nc.vector.reciprocal(rtotal[:], total[:]))
                steps.settle()
                nc.vector.tensor_tensor(af, ex, rtotal[:].unsqueeze(2).broadcast_to([P, T, E]), ALU.mult).then_inc(affinity_ready[l], 1)
                if l == 0:
                    rot_steps = Steps(dve, dve_rot)
                    rotation_angles(rot_steps)
                dve.wait_ge(affinity_turned[l], 1)
                steps.did(nc.vector.tensor_copy(work[:, 0, :], ps[0:BE, 5, :]))
                steps.settle()
                for r in range(K // 8):
                    now, then, eight = work[:, r % 2, :], work[:, (r + 1) % 2, :], slice(8 * r, 8 * r + 8)
                    steps.did(nc.vector.max(out=values[:, eight], in_=now))
                    steps.settle()
                    steps.did(nc.vector.match_replace(out=then, in_to_replace=values[:, eight], in_values=now, imm_value=LOWEST))
                    replaced = steps.n
                    steps.did(nc.vector.max_index(out=index_u[:, eight], in_max=values[:, eight], in_values=now))
                    dve.wait_ge(steps.sem, replaced)
                steps.settle()
                nc.vector.tensor_copy(index_f[:], index_u[:]).then_inc(topk_ready[l], 1)
                nc.vector.tensor_copy(index_h[:], index_u[:]).then_inc(topk_ready[l], 1)
                if l == 0:
                    rotation_rows(rot_steps)
                for b in range(B):
                    dve.wait_ge(index_all_ready[l], b + 1)
                    for c in range(C):
                        nc.vector.tensor_scalar(pick[:, b, c], index_all[:, b * E:(b + 1) * E, :], token_of_partition[:, c:c + 1],
                                                None, ALU.is_equal).then_inc(pick_ready[l], 1)

            def experts(l):
                dve.wait_ge(topkT_ready[l], 2)
                with dve.Fori(0, E // 2) as i:
                    for u in range(2):
                        e = 2 * i + u
                        dve.wait_ge(scatter_done[l], 2 * i + (u + 1))
                        for b in range(B):
                            nc.vector.tensor_scalar(place[:, u, b, :], token_row[:], indexT[:, b, bass.ds(e, 1)], None,
                                                    ALU.is_equal).then_inc(scatter_ready[l], 1)
                        for m in range(MI):
                            dve.wait_ge(silu_ready[l], i * (2 * MI) + (MI * u + m + 1))
                            dve.wait_ge(gate_up_done[l], i * (4 * MI) + (2 * MI * u + 2 * m + 2))
                            nc.vector.tensor_tensor(hidden[:, u, m, :], silu[:, m, :], ps[:, 5 - m, :], ALU.mult).then_inc(hidden_ready[l], 1)
                        dve.wait_ge(down_done[l], 2 * i + (u + 1))
                        nc.vector.tensor_tensor(weighted[:], ps[:, 7, :].rearrange("p (b d) -> p b d", b=B),
                                                gateT[:, :, bass.ds(e, 1)].broadcast_to([P, B, D]), ALU.mult).then_inc(weighted_ready[l], 1)
                        dve.wait_ge(weighted_ready[l], 2 * i + (u + 2))
                        nc.vector.tensor_copy(wy_hi[:, u], weighted[:]).then_inc(scatter_ready[l], 1)
                        dve.wait_ge(scatter_ready[l], i * (2 * (B + 2)) + ((B + 2) * u + B + 1))
                        nc.vector.tensor_tensor(wy_lo[:, u], weighted[:], wy_hi[:, u].bitcast(F32), ALU.subtract).then_inc(scatter_ready[l], 1)

            def add_moe(l, b):
                dve.wait_ge(moe_turned[l], b + 1)
                xs = x[:, b * C:(b + 1) * C, :].rearrange("p c d -> p (c d)")
                nc.vector.tensor_tensor(xs, xs, ps[:, 4 + b, :], ALU.add).then_inc(x_added[l], 1)

            steps = Steps(dve, dve_norm[0])
            for b in range(B):
                dve.wait_ge(x_loaded[b], 16)
                norm_stats(0, b, steps)
            route(0, steps)
            experts(0)

            steps = Steps(dve, dve_norm[1])
            for b in range(B):
                add_moe(0, b)
                dve.wait_ge(x_added[0], b + 1)
                norm_stats(1, b, steps)
            for b in range(B):
                norm_apply(1, b, steps)
            for b in range(B):
                for qk in range(2):
                    dve.wait_ge(qk_hi_ready, 2 * b + qk + 1)
                    if b >= 2:
                        dve.wait_ge(lo_stored[b % 2][qk], 32 * (b // 2))
                    nc.vector.tensor_tensor(part_lo[:, b % 2, qk, :], ps[:, 4 + qk, :], part_hi[:, b % 2, qk, :].bitcast(F32),
                                            ALU.subtract).then_inc(qk_lo_ready, 1)
                for w in range(2):
                    n = 2 * b + w
                    dve.wait_ge(vae_projected, n + 1)
                    nc.vector.tensor_tensor(vae[:, 2 * n:2 * n + 2, :], ps[:, 6 + w, 0:2 * (D + 2 * H)].rearrange("p (t f) -> p t f", t=2),
                                            bias_row[:].unsqueeze(1).broadcast_to([P, 2, D + 2 * H]), ALU.add).then_inc(vae_ready, 1)
            dve.wait_ge(gate_exp_ready, 1)
            nc.vector.tensor_scalar(gate_one, gate_exp, 1.0, None, ALU.add).then_inc(gate_one_ready, 1)
            dve.wait_ge(gate_one_ready, 1)
            nc.vector.reciprocal(expression[:], gate_one[:, :, H:]).then_inc(gates_ready, 1)
            nc.vector.tensor_scalar(z_weight[:], gate_one[:, :, 0:H], SUM_EPS, None, ALU.mult).then_inc(gates_ready, 1)
            dve.wait_ge(gates_ready, 2)

            def take_max(n, g, u):
                col, qt = u // C, u % C
                dve.wait_ge(max_scores_ready, n * MAX_UNITS + (u + 1))
                nc.vector.tensor_reduce(neg_max[:, g, qt, col:col + 1], ps[:, u % 2, :], AX.X, ALU.max, negate=True).then_inc(max_taken, 1)

            def norm_heads(b, g, steps):
                n = b * G + g
                dve.wait_ge(heads_turned, n + 3)
                o = ps[:, 7, :].rearrange("p (c j w) -> p c j w", c=C, j=HG)
                zw = z_weight[:, bass.ds(b * C, C), g * HG:(g + 1) * HG]
                steps.did(nc.vector.tensor_tensor(den_a[:], o[:, :, :, DH + 1], zw, ALU.mult))
                steps.settle()
                steps.did(nc.vector.tensor_tensor(den_b[:], o[:, :, :, DH], den_a[:], ALU.add))
                steps.settle()
                steps.did(nc.vector.reciprocal(den_r[:], den_b[:]))
                steps.settle()
                dst = combined[:, bass.ds(b * C, C), g * HG * DH:(g + 1) * HG * DH].rearrange("p c (j d) -> p c j d", j=HG)
                nc.vector.tensor_tensor(dst, o[:, :, :, 0:DH], den_r[:].unsqueeze(3).broadcast_to([P, C, HG, DH]),
                                        ALU.mult).then_inc(heads_normed, 1)

            for g in range(2):
                for u in range(MAX_UNITS):
                    take_max(g, g, u)

            def attend(b, last):
                steps = Steps(dve, dve_heads, b, 3 * G)
                for g in range(G):
                    n = b * G + g
                    for u in range(MAX_UNITS):
                        if not last or g < 2:
                            take_max(n + 2, (g + 2) % G, u)
                        if u == 9 and g > 0:
                            norm_heads(b, g - 1, steps)
                norm_heads(b, G - 1, steps)
                steps.end_turn()

            with dve.Fori(0, B - 1) as b:
                attend(b, False)
            attend(B - 1, True)

            steps = Steps(dve, dve_norm[2])
            for b in range(B):
                dve.wait_ge(attention_out, b + 1)
                xs = x[:, b * C:(b + 1) * C, :].rearrange("p c d -> p (c d)")
                nc.vector.tensor_tensor(xs, xs, ps[:, 4 + b, :], ALU.add).then_inc(x_attended, 1)
                dve.wait_ge(x_attended, b + 1)
                norm_stats(2, b, steps)
            route(1, steps)
            experts(1)
            for b in range(B):
                add_moe(1, b)

        @block.tensor
        def _(pe):
            def chunk(c):
                return slice(c * P, (c + 1) * P)

            def turn_xn(n, b):
                for c in range(C):
                    pe.wait_ge(xn_ready[n], C * b + c + 1)
                    last = nc.tensor.transpose(ps[:, b, chunk(c)], xn[:, C * b + c, :], ident[:])
                last.then_inc(xn_turned[n], 1)

            def route(l):
                for b in range(B):
                    turn_xn(2 * l, b)
                pe.wait_ge(gate_loaded, 16)
                for b in range(B):
                    pe.wait_ge(xnT_ready[2 * l], b + 1)
                    for c in range(C):
                        col = (c * B + b) * E
                        last = nc.tensor.matmul(ps[:, 4, col:col + E], xnT[:, b, chunk(c)], gate_sb[:], start=True, stop=True)
                last.then_inc(logits_ready[l], 1)
                pe.wait_ge(affinity_ready[l], 1)
                for c in range(C):
                    last = nc.tensor.transpose(ps[0:BE, 5, chunk(c)], affinity[:, c].rearrange("p b e -> p (b e)"), ident[:])
                last.then_inc(affinity_turned[l], 1)
                if l == 0:
                    pe.wait_ge(swap_ready, 2)
                    pe.wait_ge(attn_weights_loaded, 16 * 12)
                    nc.tensor.matmul(ps[:, 7, 0:D], swap_rows[:], wout_sb[:], start=True, stop=True).then_inc(wout_swapped, 1)
                pe.wait_ge(topk_ready[l], 2)
                nc.tensor.transpose(ps[:, 6, 0:BE], values[:], ident[0:BE, 0:BE])
                nc.tensor.transpose(ps[:, 6, BE:2 * BE], index_f[:], ident[0:BE, 0:BE]).then_inc(topk_turned[l], 1)
                for b in range(B):
                    if b >= 2:
                        pe.wait_ge(index_all_ready[l], b - 1)
                    for e in range(E):
                        last = nc.tensor.matmul(ps[:, 2 * (b % 2) + e // 4, chunk(e % 4)], row_select[:, b * E + e, :], index_h[:],
                                                start=True, stop=True)
                    last.then_inc(index_spread[l], 1)
                pe.wait_ge(topkT_ready[l], 2)
                if l == 0:
                    pe.wait_ge(rot_ready, 2)
                for b in range(B):
                    pe.wait_ge(pick_ready[l], C * (b + 1))
                    pe.wait_ge(halves_ready[l], b + 1)
                    for hf in range(2):
                        n = 2 * b + hf
                        if n >= 4:
                            pe.wait_ge(picked_ready[l], n - 3)
                        for c in range(C):
                            for half in (xn_hi, xn_lo):
                                last = nc.tensor.matmul(ps[:, 4 + n % 4, :], half[:, C * b + c, :], pick[:, b, c, 4 * hf:4 * hf + 4, :],
                                                        start=(c == 0 and half is xn_hi), stop=(c == C - 1 and half is xn_lo))
                        last.then_inc(gathered[l], 1)

            def experts(l):
                pe.wait_ge(picked_ready[l], 2 * B)
                pe.wait_ge(index_all_ready[l], B)
                for b in range(B):
                    nc.tensor.matmul(ps[:, b, :], zeros[:, 0:P], zeros[:], start=True, stop=True)

                def gate_up(e, i, u):
                    pe.wait_ge(expert_loaded[l][u], i * 48 + 48)
                    for m in range(MI):
                        cols = slice(m * P, (m + 1) * P)
                        rhs = picked[:, bass.ds(e, 1)].rearrange("p e b s -> p (e b s)")
                        nc.tensor.matmul(ps[:, 4 + 2 * m, :], wg_sb[:, u, cols], rhs, start=True, stop=True).then_inc(gate_up_done[l], 1)
                        if m == 1:
                            pe.wait_ge(silu_ready[l], i * (2 * MI) + (MI * u + 1))
                        nc.tensor.matmul(ps[:, 5 - m, :], wu_sb[:, u, cols], rhs, start=True, stop=True).then_inc(gate_up_done[l], 1)

                def down(i, u):
                    pe.wait_ge(hidden_ready[l], i * (2 * MI) + (MI * u + 2 * MI))
                    pe.wait_ge(weighted_ready[l], 2 * i + (u + 1))
                    for b in range(B):
                        for m in range(MI):
                            last = nc.tensor.matmul(ps[:, 7, chunk(b)], hidden[:, u, m, chunk(b)], wd_sb[:, u, m, :],
                                                    start=(m == 0), stop=(m == MI - 1))
                    last.then_inc(down_done[l], 1)

                def scatter(i, u, final):
                    pe.wait_ge(scatter_ready[l], i * (2 * (B + 2)) + (B + 2) * (u + 1))
                    for b in range(B):
                        nc.tensor.matmul(ps[:, b, :], wy_hi[:, u, b, :], place[:, u, b, :], start=False, stop=False, skip_group_check=True)
                        last = nc.tensor.matmul(ps[:, b, :], wy_lo[:, u, b, :], place[:, u, b, :], start=False, stop=final, skip_group_check=True)
                        if final:
                            last.then_inc(scattered[l], 1)
                    if not final:
                        last.then_inc(scatter_done[l], 1)

                gate_up(0, 0, 0)
                with pe.Fori(0, E // 2 - 1) as i:
                    down(i, 0)
                    gate_up(2 * i + 1, i, 1)
                    scatter(i, 0, False)
                    down(i, 1)
                    gate_up(2 * i + 2, i + 1, 0)
                    scatter(i, 1, False)
                i = E // 2 - 1
                down(i, 0)
                gate_up(2 * i + 1, i, 1)
                scatter(i, 0, False)
                down(i, 1)
                scatter(i, 1, True)
                pe.wait_ge(weighted_ready[l], E + 1)
                for b in range(B):
                    pe.wait_ge(moeT_ready[l], b + 1)
                    for c in range(C):
                        last = nc.tensor.transpose(ps[:, 4 + b, chunk(c)], moeT[:, b, chunk(c)], ident[:])
                    last.then_inc(moe_turned[l], 1)

            pe.wait_ge(consts_made, 10)
            route(0)
            experts(0)

            for b in range(B):
                turn_xn(1, b)
            pe.wait_ge(x_added[0], B)
            for b in range(B):
                pe.wait_ge(xnT_ready[1], b + 1)
                for qk, w in enumerate((wi_sb, wo_sb)):
                    if b > 0:
                        pe.wait_ge(qk_lo_ready, 2 * (b - 1) + qk + 1)
                    nc.tensor.matmul(ps[:, 4 + qk, :], w[:], xnT[:, b, :], start=True, stop=True).then_inc(qk_projected, 1)
                for w in range(2):
                    if b > 0:
                        pe.wait_ge(vae_ready, 2 * (b - 1) + w + 1)
                    for c in range(2):
                        f = slice(c * (D + 2 * H), (c + 1) * (D + 2 * H))
                        last = nc.tensor.matmul(ps[:, 6 + w, f], xnT[:, b, chunk(2 * w + c)], wvae_sb[:], start=True, stop=True)
                    last.then_inc(vae_projected, 1)
            pe.wait_ge(vae_ready, 2 * B)
            pe.wait_ge(qk_lo_ready, 2 * B)

            def max_scores(n, g, u):
                col, qt = u // C, u % C
                jj, pp = col // 2, col % 2
                pe.wait_ge(max_taken, n * MAX_UNITS + (u + 1))
                nc.tensor.matmul(ps[:, u % 2, :], q_stack[:, g, pp, chunk(qt)], k_stack[:, g, 2 * pp + jj, :],
                                 start=True, stop=True).then_inc(max_scores_ready, 1)

            def turn_max(n, g, normed):
                pe.wait_ge(max_taken, n * MAX_UNITS + (MAX_UNITS + 2))
                pe.wait_ge(heads_normed, normed + 1)
                for qt in range(C):
                    last = nc.tensor.transpose(ps[0:HG, 7, chunk(qt)], neg_max[:, g, qt, :], ident[:])
                last.then_inc(max_turned, 1)

            def scores(n, g, k):
                cp, j = k // 4, k % 4
                pe.wait_ge(probs_ready, n * EXP_UNITS + (k + 1))
                for cc in range(2):
                    last = nc.tensor.matmul(ps[:, 2 + 2 * (k % 2) + cc, :], k_stack[:, g, j, chunk(2 * cp + cc)], q_stack[:, g, j // 2, :],
                                            start=True, stop=True)
                last.then_inc(scores_ready, 1)
                return last

            def products(n, g, cp):
                pe.wait_ge(probs_ready, n * EXP_UNITS + (4 * cp + 4 + 2))
                if cp == 0:
                    pe.wait_ge(values_ready, 2 * n + 2)
                    pe.wait_ge(heads_copied, n + 1)
                for cc in range(2):
                    for j in range(HG):
                        last = nc.tensor.matmul(ps[32 * j:32 * j + 32, 6, :], v_ext[:, g, 2 * cp + cc, j, :], probs[:, 4 * cp + j, cc, :],
                                                start=(cp == 0 and cc == 0), stop=(cp == 1 and cc == 1))
                last.then_inc(probs_used, 1)

            def turn_heads(n, g, rows):
                pe.wait_ge(heads_copied, n + 2)
                pe.wait_ge(max_rows_ready, rows)
                pe.wait_ge(heads_normed, n + 1)
                for qt in range(C):
                    last = nc.tensor.transpose(ps[:, 7, chunk(qt)], heads_out[:, g % 2, chunk(qt)], ident[:])
                last.then_inc(heads_turned, 1)

            def attend(b, last):
                for g in range(G):
                    n = b * G + g
                    pe.wait_ge(max_rows_loaded[g], b * 32 + 32)
                    has_max = not last or g < 2
                    if has_max:
                        pe.wait_ge(stacks_loaded[(g + 2) % G], (b if g < 2 else b + 1) * 96 + 96)
                    u = 0
                    for k in range(EXP_UNITS):
                        scores(n, g, k)
                        if k == 0 and not (last and g == G - 1):
                            turn_max(n + 1, (g + 1) % G, b * G + max(g - 1, 0))
                        if k == 4 and g > 0:
                            turn_heads(n - 1, g - 1, n + (1 if last and g == G - 1 else 2))
                        if k == 5:
                            products(n, g, 0)
                        for _ in range(MAX_AFTER[k] if has_max else 0):
                            max_scores(n + 2, (g + 2) % G, u)
                            u += 1
                    products(n, g, 1)
                turn_heads(b * G + (G - 1), G - 1, b * G + (G if last else G + 1))

            for n in range(2):
                pe.wait_ge(stacks_loaded[n], 96)
                for u in range(MAX_UNITS):
                    max_scores(n, n, u)
                if n == 0:
                    turn_max(0, 0, 0)
            with pe.Fori(0, B - 1) as b:
                attend(b, False)
            attend(B - 1, True)

            pe.wait_ge(heads_normed, B * G + 1)
            for b in range(B):
                for c in range(C):
                    last = nc.tensor.transpose(ps[:, b, chunk(c)], combined[:, C * b + c, :], ident[:])
                last.then_inc(combined_turned, 1)
            for b in range(B):
                pe.wait_ge(combinedT_ready, b + 1)
                for c in range(C):
                    last = nc.tensor.matmul(ps[:, 4 + b, chunk(c)], combinedT[:, b, chunk(c)], w_rot[:], start=True, stop=True)
                last.then_inc(attention_out, 1)

            route(1)
            experts(1)


_INS = ["L0_attn_x", "L0_attn_Wa", "L0_attn_ba", "L0_attn_We", "L0_attn_be", "L0_attn_Wi", "L0_attn_Wo", "L0_attn_Wv",
        "L0_attn_Wout", "L0_attn_chi", "L0_attn_beta_p", "L0_attn_iv_p", "L0_attn_ov_p", "L0_ffn_gate_w", "L0_ffn_Wg",
        "L0_ffn_Wu", "L0_ffn_Wd"]
_OUTS = [((4, 512, 128), "float32")]


def kernel(**inputs):
    import numpy as _np
    import concourse.bacc as _bacc
    from concourse import mybir as _mybir
    from concourse.bass_utils import run_bass_kernel_spmd as _run

    nc = _bacc.Bacc("TRN2", target_bir_lowering=False, num_devices=1)
    arrays, args = {}, []
    for name in _INS:
        a = _np.ascontiguousarray(inputs[name])
        arrays[f"in_{name}_dram"] = a
        args.append(nc.dram_tensor(f"in_{name}_dram", a.shape, _mybir.dt.from_np(a.dtype), kind="ExternalInput").ap())
    for i, (shape, dtype) in enumerate(_OUTS):
        dt = _mybir.dt.from_np(_np.dtype(dtype))
        args.append(nc.dram_tensor(f"out_{i}_dram", shape, dt, kind="ExternalOutput").ap())
    macaron_block(nc, *args)
    r = _run(nc, [arrays], core_ids=[0])
    got = tuple(r.results[0][f"out_{i}_dram"] for i in range(len(_OUTS)))
    return got[0]
```

```python
import math
from contextlib import ExitStack

import concourse.bass as bass
from concourse import mybir

P = 128
F32 = mybir.dt.float32
F32R = mybir.dt.float32r
F16 = mybir.dt.float16
BF16 = mybir.dt.bfloat16
U32 = mybir.dt.uint32
I32 = mybir.dt.int32
ALU = mybir.AluOpType
ACT = mybir.ActivationFunctionType
AX = mybir.AxisListType

LOWEST = -3.0e38
LN_EPS = 1e-5
SUM_EPS = 1e-8


class Steps:

    def __init__(self, eng, sem, turn=0, per=0):
        self.eng, self.sem, self.before, self.n, self.per = eng, sem, turn * per, 0, per

    def did(self, ins):
        self.n += 1
        ins.then_inc(self.sem, 1)

    def settle(self):
        self.eng.wait_ge(self.sem, self.before + self.n)

    def end_turn(self):
        assert self.n == self.per, (self.n, self.per)


def macaron_block(nc, x_in, Wa, ba, We, be, Wi, Wo, Wv, Wout, chi, beta_p, iv_p, ov_p, gate_w, Wg, Wu, Wd, out):
    B, S, D = x_in.shape
    H = Wa.shape[1]
    DH = D // H
    E, _, I = Wg.shape
    K = max(1, int(S / E * 2))
    C = S // P
    CL = C // 2
    T = B * C
    BE = B * E
    MI = I // P
    G = 4
    HG = H // G
    PAIRS = HG // 2
    VW = 32
    SCORE_SCALE = 1.0 / math.sqrt(DH)
    assert D == P and K == P and S == 512 and DH == 8 and H == 16 and MI == 2 and E == 8 and BE == 32

    with ExitStack() as ctx:
        def sb(name, shape, dt=F32):
            return ctx.enter_context(nc.sbuf_tensor(name, shape, dt))

        def sem(name):
            return ctx.enter_context(nc.semaphore(name))

        ident = sb("ident", [P, P])
        zeros = sb("zeros", [P, S], F16)
        token_row = sb("token_row", [P, S])
        slot_row = sb("slot_row", [P, K], F16)
        earlier = sb("earlier", [P, P], F16)
        ones = sb("ones", [P, P], F16)
        gate_sb = sb("gate_sb", [P, E])
        wi_sb = sb("wi_sb", [P, D])
        wo_sb = sb("wo_sb", [P, D])
        wvae_sb = sb("wvae_sb", [P, D + 2 * H])
        bias_row = sb("bias_row", [P, D + 2 * H])
        wout_sb = sb("wout_sb", [P, D])
        swap_rows = sb("swap_rows", [P, P])
        head_params = sb("head_params", [P, 4])
        wg_sb = sb("wg_sb", [P, 2, I])
        wu_sb = sb("wu_sb", [P, 2, I])
        wd_sb = sb("wd_sb", [P, 2, MI, D])
        x = sb("x", [P, T, D])
        xn = sb("xn", [P, T, D])
        xn_hi = sb("xn_hi", [P, T, D], F16)
        xn_lo = sb("xn_lo", [P, T, D], F16)
        xnT = sb("xnT", [P, B, S])
        stats = sb("stats", [P, T, 6])
        mean_var = sb("mean_var", [P, T, 2])
        std = sb("std", [P, T])
        rstd = sb("rstd", [P, T])
        top = sb("top", [P, T])
        shifted = sb("shifted", [P, CL, 2, B, E])
        expo = sb("expo", [P, CL, 2, B, E])
        total = sb("total", [P, T])
        rtotal = sb("rtotal", [P, T])
        affinity = sb("affinity", [P, CL, 2, B, E])
        values = sb("values", [2 * BE, K])
        flipped = sb("flipped", [BE, K])
        threshold = sb("threshold", [BE, 1])
        threshold_row = sb("threshold_row", [BE, P])
        marks = sb("marks", [P, 2, C, BE], F16)
        equals_left = sb("equals_left", [P, BE])
        equal_taken = sb("equal_taken", [P, C, BE])
        taken = sb("taken", [P, C, BE])
        equals_before = sb("equals_before", [P, C, BE])
        slot_before = sb("slot_before", [P, C, BE])
        slot = sb("slot", [P, C, BE], F16)
        residue = sb("residue", [P, 2, CL, 2, B, E])
        facts = sb("facts", [P, C, B, E, 5], BF16)
        gateT = sb("gateT", [P, B, E])
        indexT = sb("indexT", [P, B, E])
        hidden = sb("hidden", [P, 2, MI, B * K])
        weighted = sb("weighted", [P, B, D])
        part_hi = sb("part_hi", [P, 2, 2, S], F32R)
        part_lo = sb("part_lo", [P, 2, 2, S], F32R)
        vae_and_gates = sb("vae_and_gates", [P, E * B * K])
        v_end, g_end = T * (D + 2 * H), T * (D + 4 * H)
        vae = vae_and_gates[:, 0:v_end].rearrange("p (t f) -> p t f", t=T)
        gate_exp = vae_and_gates[:, v_end:g_end].rearrange("p (t f) -> p t f", t=T)
        gate_one = vae_and_gates[:, g_end:g_end + T * 2 * H].rearrange("p (t f) -> p t f", t=T)
        expression = sb("expression", [P, T, H])
        z_weight = sb("z_weight", [P, T, H])
        q_stack = sb("q_stack", [P, G, PAIRS, S], F32R)
        k_stack = sb("k_stack", [P, G, HG, S], F32R)
        v_ext = sb("v_ext", [P, G, C, HG, VW])
        neg_max = sb("neg_max", [P, G, C, HG])
        max_rows = sb("max_rows", [HG, 2, S], F32R)
        probs = sb("probs", [P, 8, 2, S])
        pick = probs[:].rearrange("p k c s -> p (k c s)").bitcast(F16).rearrange("p (b c e s) -> p b c e s", b=B, c=C, e=E)
        heads_out = sb("heads_out", [P, 2, S])
        work = heads_out[0:2 * BE, :, 0:S // 2]
        den_a = sb("den_a", [P, C, HG])
        den_b = sb("den_b", [P, C, HG])
        den_r = sb("den_r", [P, C, HG])
        combined = sb("combined", [P, T, D])
        combinedT = xnT
        picked = vae_and_gates[:].rearrange("p (e b s) -> p e b s", e=E, b=B)
        silu = heads_out
        wy_hi = part_hi[:].rearrange("p u q (b d) -> p u (q b) d", d=D)[:, :, 0:B]
        wy_lo = part_hi[:].rearrange("p u q (b d) -> p u (q b) d", d=D)[:, :, B:2 * B]
        place = q_stack[:].rearrange("p (u b) q s -> p u (b q) s", u=2)
        moeT = combined[:].rearrange("p (b c) d -> p b (c d)", b=B)
        w_rot = sb("w_rot", [P, D])
        hp = sb("hp", [P, 16])
        row_i = sb("row_i", [P, 2], I32)
        parts_dram = nc.dram_tensor("parts_dram", [2, B, H, DH, 4, S], F32, kind="Internal").ap()
        zero_rows_dram = nc.dram_tensor("zero_rows_dram", [PAIRS, S], F32, kind="Internal").ap()

        ps = ctx.enter_context(nc.psum_tensor("ps", [P, 8, 512], F32))

        consts_made = sem("consts_made")
        pool_consts = sem("pool_consts")
        ident_made = sem("ident_made")
        attention_consts = sem("attention_consts")
        x_loaded = [sem(f"x_loaded{b}") for b in range(B)]
        gate_loaded = sem("gate_loaded")
        attn_weights_loaded = sem("attn_weights_loaded")
        zero_rows_stored = sem("zero_rows_stored")
        out_stored = sem("out_stored")

        def by(n, name):
            return [sem(f"{name}{i}") for i in range(n)]

        dve_norm, var_ready, std_ready = by(3, "dve_norm"), by(3, "var_ready"), by(3, "std_ready")
        xn_ready, xn_turned, xnT_ready = by(3, "xn_ready"), by(3, "xn_turned"), by(3, "xnT_ready")
        pool_halves, halves_ready = by(2, "pool_halves"), by(2, "halves_ready")
        logits_ready, dve_route, shifted_ready = by(2, "logits_ready"), by(2, "dve_route"), by(2, "shifted_ready")
        exp_ready, affinity_ready, affinity_turned = by(2, "exp_ready"), by(2, "affinity_ready"), by(2, "affinity_turned")
        threshold_ready, threshold_turned = by(2, "threshold_ready"), by(2, "threshold_turned")
        marks_ready, marks_counted, pool_facts, facts_ready = (
            by(2, "marks_ready"), by(2, "marks_counted"), by(2, "pool_facts"), by(2, "facts_ready"))
        pick_ready, gathered, picked_ready = by(2, "pick_ready"), by(2, "gathered"), by(2, "picked_ready")
        facts_gathered, slot_facts_ready = by(2, "facts_gathered"), by(2, "slot_facts_ready")
        expert_loaded = [by(2, f"expert_loaded{l}_") for l in range(2)]
        gate_up_done, silu_ready = by(2, "gate_up_done"), by(2, "silu_ready")
        hidden_ready = by(2, "hidden_ready")
        down_done = by(2, "down_done")
        weighted_ready = by(2, "weighted_ready")
        scatter_ready = by(2, "scatter_ready")
        scatter_done = by(2, "scatter_done")
        scattered, moeT_ready = by(2, "scattered"), by(2, "moeT_ready")
        moe_turned, x_added = by(2, "moe_turned"), by(2, "x_added")
        qk_projected, qk_hi_ready, qk_lo_ready = sem("qk_projected"), sem("qk_hi_ready"), sem("qk_lo_ready")
        hi_stored, lo_stored = ([by(2, f"{name}_stored{u}_") for u in range(2)] for name in ("hi", "lo"))
        vae_projected, vae_ready = sem("vae_projected"), sem("vae_ready")
        gate_exp_ready, gate_one_ready, gates_ready = sem("gate_exp_ready"), sem("gate_one_ready"), sem("gates_ready")
        swap_ready, wout_swapped, dve_rot, act_rot, rot_ready = (
            sem("swap_ready"), sem("wout_swapped"), sem("dve_rot"), sem("act_rot"), sem("rot_ready"))
        stacks_loaded, max_rows_loaded = by(G, "stacks_loaded"), by(G, "max_rows_loaded")
        max_scores_ready = sem("max_scores_ready")
        max_taken = sem("max_taken")
        max_turned, max_rows_ready = sem("max_turned"), sem("max_rows_ready")
        scores_ready = sem("scores_ready")
        probs_ready = sem("probs_ready")
        probs_used = sem("probs_used")
        values_ready = sem("values_ready")
        heads_copied = sem("heads_copied")
        heads_turned = sem("heads_turned")
        dve_heads = sem("dve_heads")
        heads_normed = sem("heads_normed")
        combined_turned, combinedT_ready = sem("combined_turned"), sem("combinedT_ready")
        attention_out, x_attended = sem("attention_out"), sem("x_attended")
        head_starts = [(hidden_ready[l], MI) for l in range(2)] + [(weighted_ready[l], 1) for l in range(2)] + [
            (scatter_done[l], 2) for l in range(2)] + [
            (max_taken, 2), (scores_ready, 1), (probs_ready, 2), (probs_used, 2), (heads_copied, 1),
            (heads_turned, 2), (heads_normed, 1)]

        MAX_UNITS = HG * C
        EXP_UNITS = HG * 2
        NORM_AT = 13

        block = ctx.enter_context(nc.Block())

        @block.sync
        def _(sp):
            for b in range(B):
                sp.dma_start(x[:, b * C:(b + 1) * C, :], x_in[b].rearrange("(c p) d -> p c d", p=P)).then_inc(x_loaded[b], 16)
            sp.dma_start(gate_sb[:], gate_w).then_inc(gate_loaded, 16)

            def load_expert(l, e, u):
                sp.dma_start(wg_sb[:, u:u + 1, :], Wg.rearrange("e d i -> d e i")[:, bass.ds(e, 1), :]).then_inc(expert_loaded[l][u], 16)
                sp.dma_start(wu_sb[:, u:u + 1, :], Wu.rearrange("e d i -> d e i")[:, bass.ds(e, 1), :]).then_inc(expert_loaded[l][u], 16)
                sp.dma_start(wd_sb[:, u:u + 1], Wd.rearrange("e (m p) d -> p e m d", p=P)[:, bass.ds(e, 1)]).then_inc(expert_loaded[l][u], 16)

            load_expert(0, 0, 0)
            load_expert(0, 1, 1)
            for dst, src in ((wi_sb[:], Wi), (wo_sb[:], Wo), (wvae_sb[:, 0:D], Wv), (wvae_sb[:, D:D + H], Wa),
                             (wvae_sb[:, D + H:], We), (wout_sb[:], Wout),
                             (bias_row[:, D:D + H], ba.rearrange("(a h) -> a h", a=1).broadcast_to([P, H])),
                             (bias_row[:, D + H:], be.rearrange("(a h) -> a h", a=1).broadcast_to([P, H]))):
                sp.dma_start(dst, src).then_inc(attn_weights_loaded, 16)
            for n, param in enumerate((beta_p, iv_p, ov_p, chi)):
                each_row = param.rearrange("(h r a) -> h r a", r=1, a=1).broadcast_to([H, DH, 1])
                sp.dma_start(head_params[:, n:n + 1], each_row).then_inc(attn_weights_loaded, 16)

            def load_experts(l):
                with sp.Fori(1, E // 2) as i:
                    for u in range(2):
                        sp.wait_ge(down_done[l], 2 * i + (u - 1))
                        load_expert(l, 2 * i + u, u)

            load_experts(0)
            sp.wait_ge(consts_made, 7)
            sp.dma_start(zero_rows_dram, zeros[0:PAIRS].bitcast(F32).rearrange("p (a t) -> p a t", a=1).broadcast_to([PAIRS, 2, S // 2])).then_inc(zero_rows_stored, 16)

            def store_parts(b):
                for qk in range(2):
                    blocks = parts_dram[qk, b].rearrange("h d (m n) t -> m n (h d) t", m=2)
                    for half, (parts, ready, stored) in enumerate(((part_hi, qk_hi_ready, hi_stored), (part_lo, qk_lo_ready, lo_stored))):
                        sp.wait_ge(ready, 2 * b + qk + 1)
                        twice = blocks[half] if qk == 0 else blocks[:, half]
                        sp.dma_start(twice.rearrange("n r t -> r n t"),
                                     parts[:, b % 2, qk, :].bitcast(F32).unsqueeze(1).broadcast_to([P, 2, S])).then_inc(stored[b % 2][qk], 16)

            def load_stacks(b, g):
                for qk in range(2):
                    rows = parts_dram[qk].rearrange("b (g pp jj) d a t -> g jj b (d a) pp t", g=G, pp=PAIRS)
                    for jj in range(2):
                        at = slice(64 * jj, 64 * jj + 4 * DH)
                        stack = q_stack[at, g] if qk == 0 else k_stack[at, g].rearrange("r (pp jj) t -> r jj pp t", jj=2)[:, jj]
                        sp.dma_start(stack.bitcast(F32), rows[g, jj, bass.ds(b, 1)].squeeze(0)).then_inc(stacks_loaded[g], 16)
                for jj in range(2):
                    sp.dma_start(q_stack[64 * jj + 4 * DH:64 * jj + 4 * DH + 1, g].bitcast(F32), zero_rows_dram).then_inc(stacks_loaded[g], 16)

            def load_max_rows(n, g):
                sp.wait_ge(max_rows_ready, n + 1)
                for jj in range(2):
                    sp.dma_start(q_stack[64 * jj + 32:64 * jj + 33, g].bitcast(F32),
                                 max_rows[2 * jj:2 * jj + 2, g % 2, :].bitcast(F32)).then_inc(max_rows_loaded[g], 16)

            store_parts(0)
            for qk in range(2):
                sp.wait_ge(hi_stored[0][qk], 16)
                sp.wait_ge(lo_stored[0][qk], 16)
            sp.wait_ge(zero_rows_stored, 16)
            sp.wait_ge(attention_consts, 3)
            for g in range(2):
                load_stacks(0, g)
            for b in range(1, B):
                store_parts(b)
            load_stacks(0, 2)
            load_max_rows(0, 0)
            for u in range(2):
                for qk in range(2):
                    sp.wait_ge(hi_stored[u][qk], 16 * B // 2)
                    sp.wait_ge(lo_stored[u][qk], 16 * B // 2)

            load_stacks(0, 3)
            load_max_rows(1, 1)
            with sp.Fori(0, B - 1) as b:
                for step in range(1, G + 1):
                    n = b * G + step
                    sp.wait_ge(scores_ready, n * EXP_UNITS + 1)
                    load_stacks(b + 1, (step + 3) % G)
                    load_max_rows(n + 1, (step + 1) % G)
            for step in range(1, G - 1):
                load_max_rows((B - 1) * G + step + 1, step + 1)

            sp.wait_ge(down_done[0], E)
            load_expert(1, 0, 0)
            load_expert(1, 1, 1)
            load_experts(1)
            for b in range(B):
                sp.wait_ge(x_added[1], b + 1)
                sp.dma_start(out[b].rearrange("(c p) d -> p c d", p=P), x[:, b * C:(b + 1) * C, :]).then_inc(out_stored, 16)
            sp.wait_ge(out_stored, 16 * B)

        @block.gpsimd
        def _(pool):
            for counter, start in head_starts:
                pool.sem_inc(counter, start)
            nc.gpsimd.memset(ident[:], 0.0).then_inc(pool_consts, 1)
            nc.gpsimd.memset(ones[:], 1.0).then_inc(pool_consts, 1)
            pool.wait_ge(pool_consts, 1)
            nc.gpsimd.affine_select(out=ident[:], in_=ident[:], compare_op=ALU.not_equal, fill=1.0, base=0,
                                    pattern=[[-1, P]], channel_multiplier=1).then_inc(ident_made, 1)
            pool.wait_ge(pool_consts, 2)
            nc.gpsimd.affine_select(out=earlier[:], in_=ones[:], compare_op=ALU.is_gt, fill=0.0, base=0,
                                    pattern=[[1, P]], channel_multiplier=-1).then_inc(consts_made, 1)
            nc.gpsimd.iota(slot_row[:], pattern=[[1, K]], base=1, channel_multiplier=0,
                           allow_small_or_imprecise_dtypes=True).then_inc(consts_made, 1)
            nc.gpsimd.iota(token_row[:], pattern=[[1, S]], base=0, channel_multiplier=0,
                           allow_small_or_imprecise_dtypes=True).then_inc(consts_made, 1)
            nc.gpsimd.iota(row_i[:, 0:1], pattern=[[0, 1]], base=0, channel_multiplier=1).then_inc(consts_made, 1)
            nc.gpsimd.memset(zeros[:], 0.0).then_inc(consts_made, 1)
            nc.gpsimd.iota(facts[:, :, :, :, 0], pattern=[[0, C], [0, BE]], base=0, channel_multiplier=1,
                           allow_small_or_imprecise_dtypes=True).then_inc(consts_made, 1)
            nc.gpsimd.iota(facts[:, :, :, :, 1], pattern=[[P, C], [0, BE]], base=0, channel_multiplier=0,
                           allow_small_or_imprecise_dtypes=True).then_inc(consts_made, 1)

            def attention_constants():
                nc.gpsimd.memset(bias_row[:, 0:D], 0.0).then_inc(pool_consts, 1)
                nc.gpsimd.memset(v_ext[:], 0.0).then_inc(pool_consts, 1)
                nc.gpsimd.memset(k_stack[:].bitcast(F32), 0.0).then_inc(pool_consts, 1)
                pool.wait_ge(pool_consts, 5)
                nc.gpsimd.memset(v_ext[:, :, :, :, DH + 1:DH + 2], 1.0).then_inc(attention_consts, 1)
                for jj in range(2):
                    pool.wait_ge(attention_consts, 1 + jj)
                    ones_rows = k_stack[64 * jj + 4 * DH:64 * jj + 4 * DH + 1].rearrange("r g (pp jj) t -> r g jj pp t", jj=2)[:, :, jj]
                    nc.gpsimd.memset(ones_rows.bitcast(F32), 1.0).then_inc(attention_consts, 1)

            def halves(l):
                for b in range(B):
                    t = slice(b * C, (b + 1) * C)
                    pool.wait_ge(xn_ready[2 * l], C * (b + 1))
                    nc.gpsimd.tensor_copy(xn_hi[:, t], xn[:, t]).then_inc(pool_halves[l], 1)
                    pool.wait_ge(pool_halves[l], b + 1)
                    nc.gpsimd.tensor_tensor(xn_lo[:, t], xn[:, t], xn_hi[:, t], ALU.subtract).then_inc(halves_ready[l], 1)

            def affinity_parts(l):
                parts = facts[:].rearrange("p (h cl) b e w -> p cl h (b e) w", cl=CL)
                aff = affinity[:].rearrange("p cl h b e -> p cl h (b e)")
                rest = residue[:].rearrange("p n cl h b e -> p n cl h (b e)")
                pool.wait_ge(affinity_ready[l], 1)
                sources = (aff, rest[:, 0], rest[:, 1])
                done = 0
                for n in range(3):
                    for cl in range(CL):
                        last = nc.gpsimd.tensor_copy(parts[:, cl, :, :, 2 + n], sources[n][:, cl])
                        last.then_inc(pool_facts[l] if n < 2 else facts_ready[l], 1)
                    if n < 2:
                        done += CL
                        pool.wait_ge(pool_facts[l], done)
                        for cl in range(CL):
                            nc.gpsimd.tensor_tensor(rest[:, n, cl], sources[n][:, cl], parts[:, cl, :, :, 2 + n], ALU.subtract).then_inc(pool_facts[l], 1)
                        done += CL
                        pool.wait_ge(pool_facts[l], done)

            halves(0)
            affinity_parts(0)
            attention_constants()
            pool.wait_ge(attention_consts, 3)
            pool.wait_ge(gates_ready, 2)

            def extend_values(b):
                for g in range(G):
                    if not isinstance(b, int):
                        pool.wait_ge(probs_used, b * (2 * G) + (2 * (g - G) + 4))
                    heads = slice(g * HG, (g + 1) * HG)
                    ex = expression[:, bass.ds(b * C, C), heads].unsqueeze(3)
                    v = vae[:, bass.ds(b * C, C), g * HG * DH:(g + 1) * HG * DH].rearrange("p c (j d) -> p c j d", d=DH)
                    nc.gpsimd.tensor_tensor(v_ext[:, g, :, :, 0:DH], v, ex.broadcast_to([P, C, HG, DH]), ALU.mult).then_inc(values_ready, 1)
                    nc.gpsimd.tensor_copy(v_ext[:, g, :, :, DH:DH + 1], ex).then_inc(values_ready, 1)

            extend_values(0)
            with pool.Fori(1, B) as b:
                extend_values(b)
            halves(1)
            affinity_parts(1)

        @block.scalar
        def _(act):
            def roots(n):
                for b in range(B):
                    t = slice(b * C, (b + 1) * C)
                    act.wait_ge(var_ready[n], b + 1)
                    nc.scalar.activation(std[:, t], mean_var[:, t, 1], ACT.Sqrt).then_inc(std_ready[n], 1)

            def copy_xnT(n, b):
                act.wait_ge(xn_turned[n], b + 1)
                nc.scalar.copy(xnT[:, b, :], ps[:, b, :]).then_inc(xnT_ready[n], 1)

            def rotation():
                act.wait_ge(attn_weights_loaded, 16 * 12)
                nc.scalar.activation(hp[:, 0:3], head_params[:, 0:3], ACT.Exp, scale=-1.0).then_inc(act_rot, 1)
                nc.scalar.activation(hp[:, 3:4], head_params[:, 3:4], ACT.Tanh).then_inc(act_rot, 1)
                act.wait_ge(rot_ready, 1)
                nc.scalar.activation(hp[:, 10:12], hp[:, 8:10], ACT.Sin).then_inc(act_rot, 1)

            def route(l):
                roots(2 * l)
                for b in range(B):
                    copy_xnT(2 * l, b)
                act.wait_ge(shifted_ready[l], 1)
                nc.scalar.activation(expo[:], shifted[:], ACT.Exp).then_inc(exp_ready[l], 1)
                if l == 0:
                    rotation()
                for n in range(2 * B):
                    b, first = n // 2, 4 * (n % 2)
                    act.wait_ge(gathered[l], n + 1)
                    nc.scalar.copy(picked[:, first:first + 4, b, :],
                                   ps[:, 4 + n % 4, :].rearrange("p (e s) -> p e s", e=4)).then_inc(picked_ready[l], 1)

            def experts(l):
                with act.Fori(0, E // 2) as i:
                    for u in range(2):
                        for m in range(MI):
                            act.wait_ge(gate_up_done[l], i * (4 * MI) + (2 * MI * u + 2 * m + 1))
                            act.wait_ge(hidden_ready[l], i * (2 * MI) + (MI * u + m + 1))
                            nc.scalar.activation(silu[:, m, :], ps[:, 4 + 2 * m, :], ACT.Silu).then_inc(silu_ready[l], 1)
                for b in range(B):
                    act.wait_ge(scattered[l], b + 1)
                    nc.scalar.mul(moeT[:, b, :], ps[:, b, :], 0.5).then_inc(moeT_ready[l], 1)

            route(0)
            experts(0)
            roots(1)
            for b in range(B):
                copy_xnT(1, b)
                for qk in range(2):
                    act.wait_ge(qk_projected, 2 * b + qk + 1)
                    if b >= 2:
                        act.wait_ge(hi_stored[b % 2][qk], 16 * (b // 2))
                    nc.scalar.copy(part_hi[:, b % 2, qk, :], ps[:, 4 + qk, :]).then_inc(qk_hi_ready, 1)
            act.wait_ge(vae_ready, T // 2)
            nc.scalar.activation(gate_exp, vae[:, :, D:], ACT.Exp, scale=-1.0).then_inc(gate_exp_ready, 1)

            def copy_max_rows(n, slot):
                act.wait_ge(max_turned, n + 1)
                nc.scalar.copy(max_rows[:, slot, :], ps[0:HG, 7, :]).then_inc(max_rows_ready, 1)

            copy_max_rows(0, 0)

            def copy_heads(n, slot):
                act.wait_ge(probs_used, n * 2 + 4)
                act.wait_ge(heads_turned, n + 1)
                nc.scalar.copy(heads_out[:, slot, :], ps[:, 6, :]).then_inc(heads_copied, 1)

            def attend(n, g, has_before, has_next):
                for k in range(EXP_UNITS):
                    banks = slice(2 + 2 * (k % 2), 4 + 2 * (k % 2))
                    act.wait_ge(scores_ready, n * EXP_UNITS + (k + 2))
                    act.wait_ge(probs_used, n * 2 + (k // 4 + 1))
                    nc.scalar.activation(probs[:, k].rearrange("p c s -> p (c s)"), ps[:, banks, :].rearrange("p c s -> p (c s)"),
                                         ACT.Exp, scale=SCORE_SCALE).then_inc(probs_ready, 1)
                    if k == 1 and has_next:
                        copy_max_rows(n + 1, (g + 1) % 2)
                    if k == 3 and has_before:
                        copy_heads(n - 1, (g - 1) % 2)

            attend(0, 0, False, True)
            with act.Fori(0, B - 1) as b:
                for step in range(1, G + 1):
                    attend(b * G + step, step % G, True, True)
            for step in range(1, G):
                attend((B - 1) * G + step, step, True, step < G - 1)
            copy_heads(B * G - 1, 1)
            for b in range(B):
                act.wait_ge(combined_turned, b + 1)
                nc.scalar.copy(combinedT[:, b, :], ps[:, b, :]).then_inc(combinedT_ready, 1)

            route(1)
            experts(1)

        @block.vector
        def _(dve):
            def norm_stats(n, b, steps):
                tiles = range(b * C, (b + 1) * C)
                for t in tiles:
                    steps.did(nc.vector.bn_stats(out=stats[:, t, :], in_=x[:, t, :]))
                steps.settle()
                for t in tiles:
                    steps.did(nc.vector.bn_aggr(out=mean_var[:, t, :], in_=stats[:, t, :]))
                steps.settle()
                v = mean_var[:, b * C:(b + 1) * C, 1]
                nc.vector.tensor_scalar(v, v, LN_EPS, None, ALU.add).then_inc(var_ready[n], 1)

            def norm_apply(n, b, steps):
                t0 = slice(b * C, (b + 1) * C)
                dve.wait_ge(std_ready[n], b + 1)
                steps.did(nc.vector.reciprocal(rstd[:, t0], std[:, t0]))
                steps.settle()
                for t in range(b * C, (b + 1) * C):
                    nc.vector.tensor_scalar(xn[:, t, :], x[:, t, :], mean_var[:, t, 0:1], rstd[:, t:t + 1],
                                            ALU.subtract, ALU.mult).then_inc(xn_ready[n], 1)

            def rotation_angles(steps):
                dve.wait_ge(ident_made, 1)
                dve.wait_ge(consts_made, 7)
                swapped = swap_rows[:].rearrange("p (h s q) -> p h s q", s=2, q=DH // 2)
                straight = ident[:].rearrange("p (h s q) -> p h s q", s=2, q=DH // 2)
                for s in range(2):
                    nc.vector.tensor_copy(swapped[:, :, s], straight[:, :, 1 - s]).then_inc(swap_ready, 1)
                steps.did(nc.vector.tensor_scalar(row_i[:, 1:2], row_i[:, 0:1], 4, None, ALU.bitwise_and))
                dve.wait_ge(act_rot, 2)
                steps.did(nc.vector.tensor_scalar(hp[:, 0:3], hp[:, 0:3], 1.0, None, ALU.add))
                steps.settle()
                steps.did(nc.vector.tensor_scalar(hp[:, 15:16], row_i[:, 1:2], -0.5, 1.0, ALU.mult, ALU.add))
                steps.did(nc.vector.reciprocal(hp[:, 4:7], hp[:, 0:3]))
                steps.settle()
                steps.did(nc.vector.tensor_scalar(hp[:, 8:9], hp[:, 4:5], -math.pi, math.pi / 2, ALU.mult, ALU.add))
                steps.settle()
                steps.did(nc.vector.scalar_tensor_tensor(out=hp[:, 7:8], in0=hp[:, 8:9], scalar=-1.0, in1=hp[:, 8:9],
                                                         op0=ALU.mult, op1=ALU.min))
                steps.settle()
                nc.vector.tensor_scalar(hp[:, 9:10], hp[:, 7:8], math.pi / 2, None, ALU.add).then_inc(rot_ready, 1)

            def rotation_rows(steps):
                steps.did(nc.vector.tensor_tensor(hp[:, 12:13], hp[:, 5:6], hp[:, 6:7], ALU.mult))
                steps.settle()
                steps.did(nc.vector.tensor_tensor(hp[:, 12:13], hp[:, 12:13], hp[:, 3:4], ALU.mult))
                steps.settle()
                dve.wait_ge(act_rot, 3)
                steps.did(nc.vector.tensor_tensor(hp[:, 13:14], hp[:, 12:13], hp[:, 10:11], ALU.mult))
                steps.did(nc.vector.tensor_tensor(hp[:, 14:15], hp[:, 12:13], hp[:, 11:12], ALU.mult))
                steps.settle()
                steps.did(nc.vector.tensor_tensor(hp[:, 14:15], hp[:, 14:15], hp[:, 15:16], ALU.mult))
                steps.did(nc.vector.tensor_scalar(w_rot[:], wout_sb[:], hp[:, 13:14], None, ALU.mult))
                steps.settle()
                dve.wait_ge(wout_swapped, 1)
                nc.vector.scalar_tensor_tensor(out=w_rot[:], in0=ps[:, 7, 0:D], scalar=hp[:, 14:15], in1=w_rot[:],
                                               op0=ALU.mult, op1=ALU.add).then_inc(rot_ready, 1)

            def route(l, norm_steps):
                for b in range(B):
                    norm_apply(2 * l, b, norm_steps)
                steps = Steps(dve, dve_route[l])
                logits = ps[:, 4, 0:T * E].rearrange("p (t e) -> p t e", e=E)
                sh, ex, af = (a[:].rearrange("p cl h b e -> p (cl h b) e") for a in (shifted, expo, affinity))
                dve.wait_ge(logits_ready[l], 1)
                steps.did(nc.vector.tensor_reduce(top[:], logits, AX.X, ALU.max))
                steps.settle()
                nc.vector.tensor_tensor(sh, logits, top[:].unsqueeze(2).broadcast_to([P, T, E]), ALU.subtract).then_inc(shifted_ready[l], 1)
                dve.wait_ge(exp_ready[l], 1)
                steps.did(nc.vector.tensor_reduce(total[:], ex, AX.X, ALU.add))
                steps.settle()
                steps.did(nc.vector.reciprocal(rtotal[:], total[:]))
                steps.settle()
                nc.vector.tensor_tensor(af, ex, rtotal[:].unsqueeze(2).broadcast_to([P, T, E]), ALU.mult).then_inc(affinity_ready[l], 1)
                if l == 0:
                    rot_steps = Steps(dve, dve_rot)
                    rotation_angles(rot_steps)
                dve.wait_ge(affinity_turned[l], 1)
                steps.did(nc.vector.tensor_copy(work[:, 0, :], ps[0:2 * BE, 5, 0:S // 2]))
                steps.settle()
                for r in range(K // 8):
                    now, then, eight = work[:, r % 2, :], work[:, (r + 1) % 2, :], slice(8 * r, 8 * r + 8)
                    steps.did(nc.vector.max(out=values[:, eight], in_=now))
                    steps.settle()
                    if r < K // 8 - 1:
                        steps.did(nc.vector.match_replace(out=then, in_to_replace=values[:, eight], in_values=now, imm_value=LOWEST))
                        steps.settle()
                steps.did(nc.vector.tensor_copy(flipped[:], values[BE:2 * BE, ::-1]))
                steps.settle()
                steps.did(nc.vector.tensor_tensor(flipped[:], flipped[:], values[0:BE, :], ALU.max))
                steps.settle()
                steps.did(nc.vector.tensor_reduce(threshold[:], flipped[:], AX.X, ALU.min))
                steps.settle()
                nc.vector.tensor_copy(threshold_row[:], threshold[:].broadcast_to([BE, P])).then_inc(threshold_ready[l], 1)
                if l == 0:
                    rotation_rows(rot_steps)
                dve.wait_ge(threshold_turned[l], 1)
                aff = affinity[:].rearrange("p cl h b e -> p cl h (b e)")
                for kind, op in enumerate((ALU.is_gt, ALU.is_equal)):
                    for h in range(2):
                        nc.vector.tensor_tensor(marks[:, kind, CL * h:CL * h + CL], aff[:, :, h],
                                                ps[:, 6, 0:BE].unsqueeze(1).broadcast_to([P, CL, BE]), op).then_inc(marks_ready[l], 1)
                dve.wait_ge(marks_counted[l], 1)
                before = ps[:, 0, 0:2 * (C + 1) * BE].rearrange("p (k c r) -> p k c r", k=2, c=C + 1)
                left = equals_left[:].unsqueeze(1).broadcast_to([P, C, BE])
                steps.did(nc.vector.tensor_scalar(equals_left[:], before[:, 0, C], -1.0, float(K), ALU.mult, ALU.add))
                steps.settle()
                steps.did(nc.vector.tensor_tensor(equal_taken[:], before[:, 1, 0:C], left, ALU.is_lt))
                steps.did(nc.vector.tensor_tensor(equals_before[:], before[:, 1, 0:C], left, ALU.min))
                steps.settle()
                steps.did(nc.vector.tensor_tensor(equal_taken[:], equal_taken[:], marks[:, 1], ALU.mult))
                steps.did(nc.vector.tensor_tensor(slot_before[:], before[:, 0, 0:C], equals_before[:], ALU.add))
                steps.settle()
                steps.did(nc.vector.tensor_tensor(taken[:], equal_taken[:], marks[:, 0], ALU.add))
                steps.settle()
                steps.did(nc.vector.scalar_tensor_tensor(out=slot[:], in0=slot_before[:], scalar=1.0, in1=taken[:],
                                                         op0=ALU.add, op1=ALU.mult))
                steps.settle()
                for b in range(B):
                    for c in range(C):
                        nc.vector.tensor_tensor(pick[:, b, c], slot_row[:].unsqueeze(1).broadcast_to([P, E, K]),
                                                slot[:, c, b * E:(b + 1) * E].unsqueeze(2).broadcast_to([P, E, K]),
                                                ALU.is_equal).then_inc(pick_ready[l], 1)
                dve.wait_ge(facts_gathered[l], 1)
                facts_by_slot = ps[:, 1, 0:5 * BE].rearrange("p (r w) -> p r w", w=5)
                nc.vector.tensor_reduce(indexT[:].rearrange("p b e -> p (b e)"), facts_by_slot[:, :, 0:2], AX.X, ALU.add).then_inc(slot_facts_ready[l], 1)
                nc.vector.tensor_reduce(gateT[:].rearrange("p b e -> p (b e)"), facts_by_slot[:, :, 2:5], AX.X, ALU.add).then_inc(slot_facts_ready[l], 1)

            def experts(l):
                dve.wait_ge(slot_facts_ready[l], 2)
                with dve.Fori(0, E // 2) as i:
                    for u in range(2):
                        e = 2 * i + u
                        dve.wait_ge(scatter_done[l], 2 * i + (u + 1))
                        for b in range(B):
                            nc.vector.tensor_scalar(place[:, u, b, :], token_row[:], indexT[:, b, bass.ds(e, 1)], None,
                                                    ALU.is_equal).then_inc(scatter_ready[l], 1)
                        for m in range(MI):
                            dve.wait_ge(silu_ready[l], i * (2 * MI) + (MI * u + m + 1))
                            dve.wait_ge(gate_up_done[l], i * (4 * MI) + (2 * MI * u + 2 * m + 2))
                            nc.vector.tensor_tensor(hidden[:, u, m, :], silu[:, m, :], ps[:, 5 - m, :], ALU.mult).then_inc(hidden_ready[l], 1)
                        dve.wait_ge(down_done[l], 2 * i + (u + 1))
                        nc.vector.tensor_tensor(weighted[:], ps[:, 7, :].rearrange("p (b d) -> p b d", b=B),
                                                gateT[:, :, bass.ds(e, 1)].broadcast_to([P, B, D]), ALU.mult).then_inc(weighted_ready[l], 1)
                        dve.wait_ge(weighted_ready[l], 2 * i + (u + 2))
                        nc.vector.tensor_copy(wy_hi[:, u], weighted[:]).then_inc(scatter_ready[l], 1)
                        dve.wait_ge(scatter_ready[l], i * (2 * (B + 2)) + ((B + 2) * u + B + 1))
                        nc.vector.tensor_tensor(wy_lo[:, u], weighted[:], wy_hi[:, u].bitcast(F32), ALU.subtract).then_inc(scatter_ready[l], 1)

            def add_moe(l, b):
                dve.wait_ge(moe_turned[l], b + 1)
                xs = x[:, b * C:(b + 1) * C, :].rearrange("p c d -> p (c d)")
                nc.vector.tensor_tensor(xs, xs, ps[:, 4 + b, :], ALU.add).then_inc(x_added[l], 1)

            steps = Steps(dve, dve_norm[0])
            for b in range(B):
                dve.wait_ge(x_loaded[b], 16)
                norm_stats(0, b, steps)
            route(0, steps)
            experts(0)

            steps = Steps(dve, dve_norm[1])
            for b in range(B):
                add_moe(0, b)
                dve.wait_ge(x_added[0], b + 1)
                norm_stats(1, b, steps)
            for b in range(B):
                norm_apply(1, b, steps)
            dve.wait_ge(attention_consts, 3)
            for b in range(B):
                for qk in range(2):
                    dve.wait_ge(qk_hi_ready, 2 * b + qk + 1)
                    if b >= 2:
                        dve.wait_ge(lo_stored[b % 2][qk], 16 * (b // 2))
                    nc.vector.tensor_tensor(part_lo[:, b % 2, qk, :], ps[:, 4 + qk, :], part_hi[:, b % 2, qk, :].bitcast(F32),
                                            ALU.subtract).then_inc(qk_lo_ready, 1)
                for w in range(2):
                    n = 2 * b + w
                    dve.wait_ge(vae_projected, n + 1)
                    nc.vector.tensor_tensor(vae[:, 2 * n:2 * n + 2, :], ps[:, 6 + w, 0:2 * (D + 2 * H)].rearrange("p (t f) -> p t f", t=2),
                                            bias_row[:].unsqueeze(1).broadcast_to([P, 2, D + 2 * H]), ALU.add).then_inc(vae_ready, 1)
            dve.wait_ge(gate_exp_ready, 1)
            nc.vector.tensor_scalar(gate_one, gate_exp, 1.0, None, ALU.add).then_inc(gate_one_ready, 1)
            dve.wait_ge(gate_one_ready, 1)
            nc.vector.reciprocal(expression[:], gate_one[:, :, H:]).then_inc(gates_ready, 1)
            nc.vector.tensor_scalar(z_weight[:], gate_one[:, :, 0:H], SUM_EPS, None, ALU.mult).then_inc(gates_ready, 1)
            dve.wait_ge(gates_ready, 2)

            def take_max(n, g, u):
                col, qt = u // C, u % C
                dve.wait_ge(max_scores_ready, n * MAX_UNITS + (u + 1))
                nc.vector.tensor_reduce(neg_max[:, g, qt, col:col + 1], ps[:, u % 2, :], AX.X, ALU.max, negate=True).then_inc(max_taken, 1)

            def norm_heads(b, g, steps, between):
                n = b * G + g
                dve.wait_ge(heads_turned, n + 3)
                o = ps[:, 7, :].rearrange("p (c j w) -> p c j w", c=C, j=HG)
                zw = z_weight[:, bass.ds(b * C, C), g * HG:(g + 1) * HG]
                steps.did(nc.vector.tensor_tensor(den_a[:], o[:, :, :, DH + 1], zw, ALU.mult))
                between()
                steps.settle()
                steps.did(nc.vector.tensor_tensor(den_b[:], o[:, :, :, DH], den_a[:], ALU.add))
                between()
                steps.settle()
                steps.did(nc.vector.reciprocal(den_r[:], den_b[:]))
                between()
                steps.settle()
                dst = combined[:, bass.ds(b * C, C), g * HG * DH:(g + 1) * HG * DH].rearrange("p c (j d) -> p c j d", j=HG)
                nc.vector.tensor_tensor(dst, o[:, :, :, 0:DH], den_r[:].unsqueeze(3).broadcast_to([P, C, HG, DH]),
                                        ALU.mult).then_inc(heads_normed, 1)

            def attend(b, step, steps, has_max):
                n = b * G + step
                units = iter(range(MAX_UNITS) if has_max else ())

                def take(count):
                    for _ in range(count):
                        u = next(units, None)
                        if u is not None:
                            take_max(n + 2, (step + 2) % G, u)

                take(NORM_AT)
                if step > 0:
                    norm_heads(b, step - 1, steps, lambda: take(1))
                take(MAX_UNITS)

            for g in range(2):
                for u in range(MAX_UNITS):
                    take_max(g, g, u)
            attend(0, 0, None, True)
            with dve.Fori(0, B - 1) as b:
                steps = Steps(dve, dve_heads, b, 3 * G)
                for step in range(1, G + 1):
                    attend(b, step, steps, True)
                steps.end_turn()
            steps = Steps(dve, dve_heads, B - 1, 3 * G)
            for step in range(1, G + 1):
                attend(B - 1, step, steps, step < 2)

            steps = Steps(dve, dve_norm[2])
            for b in range(B):
                dve.wait_ge(attention_out, b + 1)
                xs = x[:, b * C:(b + 1) * C, :].rearrange("p c d -> p (c d)")
                nc.vector.tensor_tensor(xs, xs, ps[:, 4 + b, :], ALU.add).then_inc(x_attended, 1)
                dve.wait_ge(x_attended, b + 1)
                norm_stats(2, b, steps)
            route(1, steps)
            experts(1)
            for b in range(B):
                add_moe(1, b)

        @block.tensor
        def _(pe):
            def chunk(c):
                return slice(c * P, (c + 1) * P)

            def turn_xn(n, b):
                for c in range(C):
                    pe.wait_ge(xn_ready[n], C * b + c + 1)
                    last = nc.tensor.transpose(ps[:, b, chunk(c)], xn[:, C * b + c, :], ident[:])
                last.then_inc(xn_turned[n], 1)

            def route(l):
                for b in range(B):
                    turn_xn(2 * l, b)
                pe.wait_ge(gate_loaded, 16)
                for b in range(B):
                    pe.wait_ge(xnT_ready[2 * l], b + 1)
                    for c in range(C):
                        col = ((c % CL * 2 + c // CL) * B + b) * E
                        last = nc.tensor.matmul(ps[:, 4, col:col + E], xnT[:, b, chunk(c)], gate_sb[:], start=True, stop=True)
                last.then_inc(logits_ready[l], 1)
                pe.wait_ge(affinity_ready[l], 1)
                for cl in range(CL):
                    last = nc.tensor.transpose(ps[0:2 * BE, 5, chunk(cl)], affinity[:, cl].rearrange("p h b e -> p (h b e)"), ident[:])
                last.then_inc(affinity_turned[l], 1)
                if l == 0:
                    pe.wait_ge(swap_ready, 2)
                    pe.wait_ge(attn_weights_loaded, 16 * 12)
                    nc.tensor.matmul(ps[:, 7, 0:D], swap_rows[:], wout_sb[:], start=True, stop=True).then_inc(wout_swapped, 1)
                pe.wait_ge(threshold_ready[l], 1)
                nc.tensor.transpose(ps[:, 6, 0:BE], threshold_row[:], ident[0:BE, 0:BE]).then_inc(threshold_turned[l], 1)
                pe.wait_ge(consts_made, 7)
                pe.wait_ge(marks_ready[l], 4)
                before = ps[:, 0, 0:2 * (C + 1) * BE].rearrange("p (k c r) -> p k c r", k=2, c=C + 1)
                nc.tensor.matmul(before[:, :, 0:1], earlier[:], marks[:, :, 0:1], start=True, stop=True, skip_group_check=True)
                nc.tensor.matmul(before[:, :, 1:C + 1], ones[:], marks[:], start=True, stop=False, skip_group_check=True)
                nc.tensor.matmul(before[:, :, 1:C], earlier[:], marks[:, :, 1:C], start=False, stop=False, skip_group_check=True)
                for lag in range(2, C + 1):
                    last = nc.tensor.matmul(before[:, :, lag:C + 1], ones[:], marks[:, :, 0:C + 1 - lag], start=False, stop=lag == C, skip_group_check=True)
                last.then_inc(marks_counted[l], 1)
                if l == 0:
                    pe.wait_ge(rot_ready, 2)
                for b in range(B):
                    pe.wait_ge(pick_ready[l], C * (b + 1))
                    pe.wait_ge(halves_ready[l], b + 1)
                    if b == 0:
                        pe.wait_ge(facts_ready[l], CL)
                    for hf in range(2):
                        n = 2 * b + hf
                        if n >= 4:
                            pe.wait_ge(picked_ready[l], n - 3)
                        for c in range(C):
                            for half in (xn_hi, xn_lo):
                                last = nc.tensor.matmul(ps[:, 4 + n % 4, :], half[:, C * b + c, :], pick[:, b, c, 4 * hf:4 * hf + 4, :],
                                                        start=(c == 0 and half is xn_hi), stop=(c == C - 1 and half is xn_lo))
                        last.then_inc(gathered[l], 1)
                    for e in range(E):
                        col = 5 * (b * E + e)
                        for c in range(C):
                            last = nc.tensor.matmul(ps[:, 1, col:col + 5], pick[:, b, c, e, :], facts[:, c, b, e, :], start=(c == 0), stop=(c == C - 1))
                last.then_inc(facts_gathered[l], 1)

            def experts(l):
                pe.wait_ge(picked_ready[l], 2 * B)
                pe.wait_ge(slot_facts_ready[l], 2)
                for b in range(B):
                    nc.tensor.matmul(ps[:, b, :], zeros[:, 0:P], zeros[:], start=True, stop=True)

                def gate_up(e, i, u):
                    pe.wait_ge(expert_loaded[l][u], i * 48 + 48)
                    for m in range(MI):
                        cols = slice(m * P, (m + 1) * P)
                        rhs = picked[:, bass.ds(e, 1)].rearrange("p e b s -> p (e b s)")
                        nc.tensor.matmul(ps[:, 4 + 2 * m, :], wg_sb[:, u, cols], rhs, start=True, stop=True).then_inc(gate_up_done[l], 1)
                        if m == 1:
                            pe.wait_ge(silu_ready[l], i * (2 * MI) + (MI * u + 1))
                        nc.tensor.matmul(ps[:, 5 - m, :], wu_sb[:, u, cols], rhs, start=True, stop=True).then_inc(gate_up_done[l], 1)

                def down(i, u):
                    pe.wait_ge(hidden_ready[l], i * (2 * MI) + (MI * u + 2 * MI))
                    pe.wait_ge(weighted_ready[l], 2 * i + (u + 1))
                    for b in range(B):
                        for m in range(MI):
                            last = nc.tensor.matmul(ps[:, 7, chunk(b)], hidden[:, u, m, chunk(b)], wd_sb[:, u, m, :],
                                                    start=(m == 0), stop=(m == MI - 1))
                    last.then_inc(down_done[l], 1)

                def scatter(i, u, final):
                    pe.wait_ge(scatter_ready[l], i * (2 * (B + 2)) + (B + 2) * (u + 1))
                    for b in range(B):
                        nc.tensor.matmul(ps[:, b, :], wy_hi[:, u, b, :], place[:, u, b, :], start=False, stop=False, skip_group_check=True)
                        last = nc.tensor.matmul(ps[:, b, :], wy_lo[:, u, b, :], place[:, u, b, :], start=False, stop=final, skip_group_check=True)
                        if final:
                            last.then_inc(scattered[l], 1)
                    if not final:
                        last.then_inc(scatter_done[l], 1)

                gate_up(0, 0, 0)
                with pe.Fori(0, E // 2 - 1) as i:
                    down(i, 0)
                    gate_up(2 * i + 1, i, 1)
                    scatter(i, 0, False)
                    down(i, 1)
                    gate_up(2 * i + 2, i + 1, 0)
                    scatter(i, 1, False)
                i = E // 2 - 1
                down(i, 0)
                gate_up(2 * i + 1, i, 1)
                scatter(i, 0, False)
                down(i, 1)
                scatter(i, 1, True)
                pe.wait_ge(weighted_ready[l], E + 1)
                for b in range(B):
                    pe.wait_ge(moeT_ready[l], b + 1)
                    for c in range(C):
                        last = nc.tensor.transpose(ps[:, 4 + b, chunk(c)], moeT[:, b, chunk(c)], ident[:])
                    last.then_inc(moe_turned[l], 1)

            pe.wait_ge(ident_made, 1)
            route(0)
            experts(0)

            for b in range(B):
                turn_xn(1, b)
            pe.wait_ge(x_added[0], B)
            for b in range(B):
                pe.wait_ge(xnT_ready[1], b + 1)
                for qk, w in enumerate((wi_sb, wo_sb)):
                    if b > 0:
                        pe.wait_ge(qk_lo_ready, 2 * (b - 1) + qk + 1)
                    nc.tensor.matmul(ps[:, 4 + qk, :], w[:], xnT[:, b, :], start=True, stop=True).then_inc(qk_projected, 1)
                for w in range(2):
                    if b > 0:
                        pe.wait_ge(vae_ready, 2 * (b - 1) + w + 1)
                    for c in range(2):
                        f = slice(c * (D + 2 * H), (c + 1) * (D + 2 * H))
                        last = nc.tensor.matmul(ps[:, 6 + w, f], xnT[:, b, chunk(2 * w + c)], wvae_sb[:], start=True, stop=True)
                    last.then_inc(vae_projected, 1)
            pe.wait_ge(vae_ready, 2 * B)
            pe.wait_ge(qk_lo_ready, 2 * B)

            def max_scores(n, g, u):
                col, qt = u // C, u % C
                jj, pp = col // 2, col % 2
                pe.wait_ge(max_taken, n * MAX_UNITS + (u + 1))
                nc.tensor.matmul(ps[:, u % 2, :], q_stack[:, g, pp, chunk(qt)], k_stack[:, g, 2 * pp + jj, :],
                                 start=True, stop=True).then_inc(max_scores_ready, 1)

            def turn_max(n, g, normed):
                pe.wait_ge(max_taken, n * MAX_UNITS + (MAX_UNITS + 2))
                if normed is not None:
                    pe.wait_ge(heads_normed, normed)
                for qt in range(C):
                    last = nc.tensor.transpose(ps[0:HG, 7, chunk(qt)], neg_max[:, g, qt, :], ident[:])
                last.then_inc(max_turned, 1)

            def scores(n, g, k):
                cp, j = k // 4, k % 4
                pe.wait_ge(probs_ready, n * EXP_UNITS + (k + 1))
                for cc in range(2):
                    last = nc.tensor.matmul(ps[:, 2 + 2 * (k % 2) + cc, :], k_stack[:, g, j, chunk(2 * cp + cc)], q_stack[:, g, j // 2, :],
                                            start=True, stop=True)
                last.then_inc(scores_ready, 1)
                return last

            def products(n, g, cp, cc):
                pe.wait_ge(probs_ready, n * EXP_UNITS + (4 * cp + 4 + 2))
                if cp == 0 and cc == 0:
                    pe.wait_ge(values_ready, 2 * n + 2)
                    pe.wait_ge(heads_copied, n + 1)
                for j in range(HG):
                    last = nc.tensor.matmul(ps[32 * j:32 * j + 32, 6, :], v_ext[:, g, 2 * cp + cc, j, :], probs[:, 4 * cp + j, cc, :],
                                            start=(cp == 0 and cc == 0), stop=(cp == 1 and cc == 1))
                if cc == 1:
                    last.then_inc(probs_used, 1)

            def turn_heads(n, g, rows):
                pe.wait_ge(heads_copied, n + 2)
                pe.wait_ge(max_rows_ready, rows)
                pe.wait_ge(heads_normed, n + 1)
                for qt in range(C):
                    last = nc.tensor.transpose(ps[:, 7, chunk(qt)], heads_out[:, g % 2, chunk(qt)], ident[:])
                last.then_inc(heads_turned, 1)

            def attend(b, step, first=False, last_batch=False):
                g, n = step % G, b * G + step
                pe.wait_ge(max_rows_loaded[g], (b + step // G) * 32 + 32)
                has_max = not last_batch or step < 2
                if has_max:
                    pe.wait_ge(stacks_loaded[(g + 2) % G], (b + (step + 2) // G) * 96 + 96)
                has_next = not last_batch or step < G - 1
                for k in range(EXP_UNITS):
                    scores(n, g, k)
                    if has_max:
                        max_scores(n + 2, (g + 2) % G, 2 * k)
                    if k == 0 and has_next:
                        turn_max(n + 1, (g + 1) % G, None if first else n)
                    if not first and k in (1, 3):
                        products(n - 1, (g - 1) % G, 1, k // 2)
                    if k in (5, 7):
                        products(n, g, 0, k // 2 - 2)
                    if not first and k == 6:
                        turn_heads(n - 1, g - 1, n + (2 if has_next else 1))
                    if has_max:
                        max_scores(n + 2, (g + 2) % G, 2 * k + 1)

            for n in range(2):
                pe.wait_ge(stacks_loaded[n], 96)
                for u in range(MAX_UNITS):
                    max_scores(n, n, u)
                if n == 0:
                    turn_max(0, 0, None)
            attend(0, 0, first=True)
            with pe.Fori(0, B - 1) as b:
                for step in range(1, G + 1):
                    attend(b, step)
            for step in range(1, G):
                attend(B - 1, step, last_batch=True)
            for cc in range(2):
                products(B * G - 1, G - 1, 1, cc)
            turn_heads(B * G - 1, G - 1, B * G)

            pe.wait_ge(heads_normed, B * G + 1)
            for b in range(B):
                for c in range(C):
                    last = nc.tensor.transpose(ps[:, b, chunk(c)], combined[:, C * b + c, :], ident[:])
                last.then_inc(combined_turned, 1)
            for b in range(B):
                pe.wait_ge(combinedT_ready, b + 1)
                for c in range(C):
                    last = nc.tensor.matmul(ps[:, 4 + b, chunk(c)], combinedT[:, b, chunk(c)], w_rot[:], start=True, stop=True)
                last.then_inc(attention_out, 1)

            route(1)
            experts(1)


_INS = ["L0_attn_x", "L0_attn_Wa", "L0_attn_ba", "L0_attn_We", "L0_attn_be", "L0_attn_Wi", "L0_attn_Wo", "L0_attn_Wv",
        "L0_attn_Wout", "L0_attn_chi", "L0_attn_beta_p", "L0_attn_iv_p", "L0_attn_ov_p", "L0_ffn_gate_w", "L0_ffn_Wg",
        "L0_ffn_Wu", "L0_ffn_Wd"]
_OUTS = [((4, 512, 128), "float32")]


def kernel(**inputs):
    import numpy as _np
    import concourse.bacc as _bacc
    from concourse import mybir as _mybir
    from concourse.bass_utils import run_bass_kernel_spmd as _run

    nc = _bacc.Bacc("TRN2", target_bir_lowering=False, num_devices=1)
    arrays, args = {}, []
    for name in _INS:
        a = _np.ascontiguousarray(inputs[name])
        arrays[f"in_{name}_dram"] = a
        args.append(nc.dram_tensor(f"in_{name}_dram", a.shape, _mybir.dt.from_np(a.dtype), kind="ExternalInput").ap())
    for i, (shape, dtype) in enumerate(_OUTS):
        dt = _mybir.dt.from_np(_np.dtype(dtype))
        args.append(nc.dram_tensor(f"out_{i}_dram", shape, dt, kind="ExternalOutput").ap())
    macaron_block(nc, *args)
    r = _run(nc, [arrays], core_ids=[0])
    got = tuple(r.results[0][f"out_{i}_dram"] for i in range(len(_OUTS)))
    return got[0]
```

```python
import math
from contextlib import ExitStack

import concourse.bass as bass
from concourse import mybir

P = 128
F32 = mybir.dt.float32
F32R = mybir.dt.float32r
F16 = mybir.dt.float16
BF16 = mybir.dt.bfloat16
U32 = mybir.dt.uint32
I32 = mybir.dt.int32
ALU = mybir.AluOpType
ACT = mybir.ActivationFunctionType
AX = mybir.AxisListType

LOWEST = -3.0e38
LN_EPS = 1e-5
SUM_EPS = 1e-8


class Steps:

    def __init__(self, eng, sem, turn=0, per=0):
        self.eng, self.sem, self.before, self.n, self.per = eng, sem, turn * per, 0, per

    def did(self, ins):
        self.n += 1
        ins.then_inc(self.sem, 1)

    def settle(self):
        self.eng.wait_ge(self.sem, self.before + self.n)

    def end_turn(self):
        assert self.n == self.per, (self.n, self.per)


def macaron_block(nc, x_in, Wa, ba, We, be, Wi, Wo, Wv, Wout, chi, beta_p, iv_p, ov_p, gate_w, Wg, Wu, Wd, out):
    B, S, D = x_in.shape
    H = Wa.shape[1]
    DH = D // H
    E, _, I = Wg.shape
    K = max(1, int(S / E * 2))
    C = S // P
    CL = C // 2
    T = B * C
    BE = B * E
    MI = I // P
    G = 4
    HG = H // G
    PAIRS = HG // 2
    VW = 32
    SCORE_SCALE = 1.0 / math.sqrt(DH)
    assert D == P and K == P and S == 512 and DH == 8 and H == 16 and MI == 2 and E == 8 and BE == 32

    with ExitStack() as ctx:
        def sb(name, shape, dt=F32):
            return ctx.enter_context(nc.sbuf_tensor(name, shape, dt))

        def sem(name):
            return ctx.enter_context(nc.semaphore(name))

        ident = sb("ident", [P, P])
        zeros = sb("zeros", [P, S], F16)
        token_row = sb("token_row", [P, S])
        slot_row = sb("slot_row", [P, K], F16)
        earlier = sb("earlier", [P, P], F16)
        ones = sb("ones", [P, P], F16)
        gate_sb = sb("gate_sb", [P, E])
        wi_sb = sb("wi_sb", [P, D])
        wo_sb = sb("wo_sb", [P, D])
        wvae_sb = sb("wvae_sb", [P, D + 2 * H])
        bias_row = sb("bias_row", [P, D + 2 * H])
        wout_sb = sb("wout_sb", [P, D])
        swap_rows = sb("swap_rows", [P, P])
        head_params = sb("head_params", [P, 4])
        w_gu = sb("w_gu", [P, 2, 2, I])
        w_hi = sb("w_hi", [P, 2, 2, I], F32R)
        w_lo = sb("w_lo", [P, 2, 2, I], F32R)
        wd_sb = sb("wd_sb", [P, 2, MI, D])
        x = sb("x", [P, T, D])
        xn = sb("xn", [P, T, D])
        xn_hi = sb("xn_hi", [P, T, D], F16)
        xn_lo = sb("xn_lo", [P, T, D], F16)
        xnT = sb("xnT", [P, B, S])
        norm_eps = sb("norm_eps", [P, 1])
        stats = sb("stats", [P, T, 6])
        mean_var = sb("mean_var", [P, T, 2])
        std = sb("std", [P, T])
        rstd = sb("rstd", [P, T])
        top = sb("top", [P, T])
        shifted = sb("shifted", [P, CL, 2, B, E])
        expo = sb("expo", [P, CL, 2, B, E])
        total = sb("total", [P, T])
        rtotal = sb("rtotal", [P, T])
        affinity = sb("affinity", [P, CL, 2, B, E])
        values = sb("values", [2 * BE, K])
        flipped = sb("flipped", [BE, K])
        threshold = sb("threshold", [BE, 1])
        threshold_row = sb("threshold_row", [BE, P])
        marks = sb("marks", [P, 2, C, BE], F16)
        equals_left = sb("equals_left", [P, BE])
        equal_taken = sb("equal_taken", [P, C, BE])
        taken = sb("taken", [P, C, BE])
        equals_before = sb("equals_before", [P, C, BE])
        slot_before = sb("slot_before", [P, C, BE])
        slot = sb("slot", [P, C, BE], F16)
        residue = sb("residue", [P, 2, CL, 2, B, E])
        facts = sb("facts", [P, C, B, E, 5], BF16)
        gateT = sb("gateT", [P, B, E])
        indexT = sb("indexT", [P, B, E])
        down_out = sb("down_out", [P, B * K])
        weighted = sb("weighted", [P, B, D])
        part_hi = sb("part_hi", [P, 2, 2, S], F32R)
        part_lo = sb("part_lo", [P, 2, 2, S], F32R)
        v_end, g_end = T * (D + 2 * H), T * (D + 4 * H)
        vae_and_gates = sb("vae_and_gates", [P, g_end + T * 2 * H])
        vae = vae_and_gates[:, 0:v_end].rearrange("p (t f) -> p t f", t=T)
        gate_exp = vae_and_gates[:, v_end:g_end].rearrange("p (t f) -> p t f", t=T)
        gate_one = vae_and_gates[:, g_end:g_end + T * 2 * H].rearrange("p (t f) -> p t f", t=T)
        expression = sb("expression", [P, T, H])
        z_weight = sb("z_weight", [P, T, H])
        q_stack = sb("q_stack", [P, G, PAIRS, S], F32R)
        k_stack = sb("k_stack", [P, G, HG, S], F32R)
        v_ext = sb("v_ext", [P, G, C, HG, VW])
        neg_max = sb("neg_max", [P, G, C, HG])
        max_rows = sb("max_rows", [HG, 2, S], F32R)
        probs = sb("probs", [P, C, HG, S])
        pick = probs[:].rearrange("p k c s -> p (k c s)").bitcast(F16).rearrange("p (b c e s) -> p b c e s", b=B, c=C, e=E)
        heads_out = sb("heads_out", [P, 2, S])
        work = heads_out[0:2 * BE, :, 0:S // 2]
        den_a = sb("den_a", [P, C, HG])
        den_b = sb("den_b", [P, C, HG])
        den_r = sb("den_r", [P, C, HG])
        combined = sb("combined", [P, T, D])
        combinedT = xnT
        picked_hi, picked_lo = (k_stack[:].rearrange("p (n g) j s -> p n (g j s)", n=2)[:, n].rearrange(
            "p (e b s) -> p e b s", e=E, b=B) for n in range(2))
        hidden = vae_and_gates[:, 0:2 * MI * B * K].rearrange("p (u m s) -> p u m s", u=2, m=MI)
        silu = heads_out
        wy_hi = part_hi[:].rearrange("p u q (b d) -> p u (q b) d", d=D)[:, :, 0:B]
        wy_lo = part_hi[:].rearrange("p u q (b d) -> p u (q b) d", d=D)[:, :, B:2 * B]
        place = q_stack[:].rearrange("p (u b) q s -> p u (b q) s", u=2)
        moeT = combined[:].rearrange("p (b c) d -> p b (c d)", b=B)
        w_rot = sb("w_rot", [P, D])
        hp = sb("hp", [P, 16])
        row_i = sb("row_i", [P, 2], I32)
        parts_dram = nc.dram_tensor("parts_dram", [2, B, H, DH, 4, S], F32, kind="Internal").ap()
        zero_rows_dram = nc.dram_tensor("zero_rows_dram", [PAIRS, S], F32, kind="Internal").ap()

        ps = ctx.enter_context(nc.psum_tensor("ps", [P, 8, 512], F32))

        consts_made = sem("consts_made")
        pool_consts = sem("pool_consts")
        ident_made = sem("ident_made")
        eps_made = sem("eps_made")
        attention_consts = sem("attention_consts")
        x_loaded = [sem(f"x_loaded{b}") for b in range(B)]
        gate_loaded = sem("gate_loaded")
        attn_weights_loaded = sem("attn_weights_loaded")
        zero_rows_stored = sem("zero_rows_stored")
        out_stored = sem("out_stored")

        def by(n, name):
            return [sem(f"{name}{i}") for i in range(n)]

        dve_norm, var_ready, std_ready = by(3, "dve_norm"), by(3, "var_ready"), by(3, "std_ready")
        xn_ready, xn_turned, xnT_ready = by(3, "xn_ready"), by(3, "xn_turned"), by(3, "xnT_ready")
        pool_halves, halves_ready = by(2, "pool_halves"), by(2, "halves_ready")
        logits_ready, dve_route, shifted_ready = by(2, "logits_ready"), by(2, "dve_route"), by(2, "shifted_ready")
        exp_ready, affinity_ready, affinity_turned = by(2, "exp_ready"), by(2, "affinity_ready"), by(2, "affinity_turned")
        threshold_ready, threshold_turned = by(2, "threshold_ready"), by(2, "threshold_turned")
        marks_ready, marks_counted, pool_facts, facts_ready = (
            by(2, "marks_ready"), by(2, "marks_counted"), by(2, "pool_facts"), by(2, "facts_ready"))
        slot_ready = by(2, "slot_ready")
        pick_ready, gathered, picked_ready = by(2, "pick_ready"), by(2, "gathered"), by(2, "picked_ready")
        facts_gathered, slot_facts_ready = by(2, "facts_gathered"), by(2, "slot_facts_ready")
        expert_loaded = [by(2, f"expert_loaded{l}_") for l in range(2)]
        w_hi_ready, w_lo_ready = by(2, "w_hi_ready"), by(2, "w_lo_ready")
        gate_up_done, silu_ready = by(2, "gate_up_done"), by(2, "silu_ready")
        hidden_ready = by(2, "hidden_ready")
        down_done = by(2, "down_done")
        down_copied, down_turned = by(2, "down_copied"), by(2, "down_turned")
        weighted_ready = by(2, "weighted_ready")
        place_ready = by(2, "place_ready")
        scatter_ready = by(2, "scatter_ready")
        scatter_done = by(2, "scatter_done")
        scattered, moeT_ready = by(2, "scattered"), by(2, "moeT_ready")
        moe_turned, x_added = by(2, "moe_turned"), by(2, "x_added")
        qk_projected, qk_hi_ready, qk_lo_ready = sem("qk_projected"), sem("qk_hi_ready"), sem("qk_lo_ready")
        hi_stored, lo_stored = ([by(2, f"{name}_stored{u}_") for u in range(2)] for name in ("hi", "lo"))
        vae_projected, vae_ready = sem("vae_projected"), sem("vae_ready")
        gate_exp_ready, gate_one_ready, gates_ready = sem("gate_exp_ready"), sem("gate_one_ready"), sem("gates_ready")
        swap_ready, wout_swapped, dve_rot, act_rot, rot_ready = (
            sem("swap_ready"), sem("wout_swapped"), sem("dve_rot"), sem("act_rot"), sem("rot_ready"))
        stacks_loaded, max_rows_loaded = by(G, "stacks_loaded"), by(G, "max_rows_loaded")
        max_scores_ready = sem("max_scores_ready")
        max_taken = sem("max_taken")
        max_turned, max_rows_ready = sem("max_turned"), sem("max_rows_ready")
        scores_ready = sem("scores_ready")
        probs_ready = sem("probs_ready")
        probs_used = sem("probs_used")
        values_ready = sem("values_ready")
        heads_copied = sem("heads_copied")
        heads_turned = sem("heads_turned")
        dve_heads = sem("dve_heads")
        heads_normed = sem("heads_normed")
        combined_turned, combinedT_ready = sem("combined_turned"), sem("combinedT_ready")
        attention_out, x_attended = sem("attention_out"), sem("x_attended")
        RING = 3
        head_starts = [(hidden_ready[l], MI) for l in range(2)] + [(weighted_ready[l], 1) for l in range(2)] + [
            (scatter_done[l], 2) for l in range(2)] + [
            (max_taken, RING), (scores_ready, 1), (probs_ready, RING), (probs_used, C), (heads_copied, 1),
            (heads_turned, 2), (heads_normed, 1)]

        MAX_UNITS = HG * C
        EXP_UNITS = C * HG

        def ring_bank(step, u):
            return (MAX_UNITS * step + u) % RING

        def ring_wait(n, step, u, first_step):
            return n * MAX_UNITS + (u + 1 + (RING - 1 if step == first_step and u == 0 else 0))
        TURN_BANK, OUT_BANK = (0, 0, 0, 4), (1, 1, 1, 5)
        HEADS_AT, TURN_AT = 3, 4
        NORM_AT = 9

        def after(i, o, per, more=0):
            return i * (2 * per) + (per * o + more)

        def pick_bank(n):
            return 2 + 2 * (n % 3)

        block = ctx.enter_context(nc.Block())

        @block.sync
        def _(sp):
            for b in range(B):
                sp.dma_start(x[:, b * C:(b + 1) * C, :], x_in[b].rearrange("(c p) d -> p c d", p=P)).then_inc(x_loaded[b], 16)
            sp.dma_start(gate_sb[:], gate_w).then_inc(gate_loaded, 16)

            def load_expert(l, e, u):
                sp.dma_start(w_gu[:, u:u + 1, 0, :], Wg.rearrange("e d i -> d e i")[:, bass.ds(e, 1), :]).then_inc(expert_loaded[l][u], 16)
                sp.dma_start(w_gu[:, u:u + 1, 1, :], Wu.rearrange("e d i -> d e i")[:, bass.ds(e, 1), :]).then_inc(expert_loaded[l][u], 16)
                sp.dma_start(wd_sb[:, u:u + 1], Wd.rearrange("e (m p) d -> p e m d", p=P)[:, bass.ds(e, 1)]).then_inc(expert_loaded[l][u], 16)

            load_expert(0, 0, 0)
            load_expert(0, 1, 1)
            for dst, src in ((wi_sb[:], Wi), (wo_sb[:], Wo), (wvae_sb[:, 0:D], Wv), (wvae_sb[:, D:D + H], Wa),
                             (wvae_sb[:, D + H:], We), (wout_sb[:], Wout),
                             (bias_row[:, D:D + H], ba.rearrange("(a h) -> a h", a=1).broadcast_to([P, H])),
                             (bias_row[:, D + H:], be.rearrange("(a h) -> a h", a=1).broadcast_to([P, H]))):
                sp.dma_start(dst, src).then_inc(attn_weights_loaded, 16)
            for n, param in enumerate((beta_p, iv_p, ov_p, chi)):
                each_row = param.rearrange("(h r a) -> h r a", r=1, a=1).broadcast_to([H, DH, 1])
                sp.dma_start(head_params[:, n:n + 1], each_row).then_inc(attn_weights_loaded, 16)

            def load_experts(l):
                with sp.Fori(1, E // 2) as i:
                    for u in range(2):
                        sp.wait_ge(down_done[l], 2 * i + (u - 1))
                        load_expert(l, 2 * i + u, u)

            load_experts(0)
            sp.wait_ge(consts_made, 7)
            sp.dma_start(zero_rows_dram, zeros[0:PAIRS].bitcast(F32).rearrange("p (a t) -> p a t", a=1).broadcast_to([PAIRS, 2, S // 2])).then_inc(zero_rows_stored, 16)

            def store_parts(b):
                for half, (parts, ready, stored) in enumerate(((part_hi, qk_hi_ready, hi_stored), (part_lo, qk_lo_ready, lo_stored))):
                    for qk in range(2):
                        blocks = parts_dram[qk, b].rearrange("h d (m n) t -> m n (h d) t", m=2)
                        sp.wait_ge(ready, 2 * b + qk + 1)
                        twice = blocks[half] if qk == 0 else blocks[:, half]
                        sp.dma_start(twice.rearrange("n r t -> r n t"),
                                     parts[:, b % 2, qk, :].bitcast(F32).unsqueeze(1).broadcast_to([P, 2, S])).then_inc(stored[b % 2][qk], 16)

            def load_stacks(b, g):
                for qk in range(2):
                    rows = parts_dram[qk].rearrange("b (g pp jj) d a t -> g jj b (d a) pp t", g=G, pp=PAIRS)
                    for jj in range(2):
                        at = slice(64 * jj, 64 * jj + 4 * DH)
                        stack = q_stack[at, g] if qk == 0 else k_stack[at, g].rearrange("r (pp jj) t -> r jj pp t", jj=2)[:, jj]
                        sp.dma_start(stack.bitcast(F32), rows[g, jj, bass.ds(b, 1)].squeeze(0)).then_inc(stacks_loaded[g], 16)

            def clear_max_rows(g):
                for jj in range(2):
                    sp.dma_start(q_stack[64 * jj + 4 * DH:64 * jj + 4 * DH + 1, g].bitcast(F32), zero_rows_dram).then_inc(stacks_loaded[g], 16)

            def load_max_rows(n, g):
                sp.wait_ge(max_rows_ready, n + 1)
                for jj in range(2):
                    sp.dma_start(q_stack[64 * jj + 32:64 * jj + 33, g].bitcast(F32),
                                 max_rows[2 * jj:2 * jj + 2, g % 2, :].bitcast(F32)).then_inc(max_rows_loaded[g], 16)

            sp.wait_ge(scattered[0], B)
            sp.wait_ge(zero_rows_stored, 16)
            sp.wait_ge(attention_consts, 3)
            for g in range(G):
                clear_max_rows(g)
            store_parts(0)
            for qk in range(2):
                sp.wait_ge(hi_stored[0][qk], 16)
                sp.wait_ge(lo_stored[0][qk], 16)
            load_stacks(0, 0)
            store_parts(1)
            for g in range(1, G):
                load_stacks(0, g)
            load_max_rows(0, 0)
            store_parts(2)
            store_parts(3)
            load_max_rows(1, 1)
            for u in range(2):
                for qk in range(2):
                    sp.wait_ge(hi_stored[u][qk], 16 * B // 2)
                    sp.wait_ge(lo_stored[u][qk], 16 * B // 2)
            with sp.Fori(0, B - 1) as b:
                for step in range(1, G + 1):
                    n = b * G + step
                    sp.wait_ge(scores_ready, n * EXP_UNITS + 1)
                    clear_max_rows((step + 3) % G)
                    load_stacks(b + 1, (step + 3) % G)
                    load_max_rows(n + 1, (step + 1) % G)
            for step in range(1, G - 1):
                load_max_rows((B - 1) * G + step + 1, step + 1)

            sp.wait_ge(down_done[0], E)
            load_expert(1, 0, 0)
            load_expert(1, 1, 1)
            load_experts(1)
            for b in range(B):
                sp.wait_ge(x_added[1], b + 1)
                sp.dma_start(out[b].rearrange("(c p) d -> p c d", p=P), x[:, b * C:(b + 1) * C, :]).then_inc(out_stored, 16)
            sp.wait_ge(out_stored, 16 * B)

        @block.gpsimd
        def _(pool):
            for counter, start in head_starts:
                pool.sem_inc(counter, start)
            nc.gpsimd.memset(norm_eps[:], LN_EPS).then_inc(eps_made, 1)
            nc.gpsimd.memset(ident[:], 0.0).then_inc(pool_consts, 1)
            nc.gpsimd.memset(ones[:], 1.0).then_inc(pool_consts, 1)
            pool.wait_ge(pool_consts, 1)
            nc.gpsimd.affine_select(out=ident[:], in_=ident[:], compare_op=ALU.not_equal, fill=1.0, base=0,
                                    pattern=[[-1, P]], channel_multiplier=1).then_inc(ident_made, 1)
            pool.wait_ge(pool_consts, 2)
            nc.gpsimd.affine_select(out=earlier[:], in_=ones[:], compare_op=ALU.is_gt, fill=0.0, base=0,
                                    pattern=[[1, P]], channel_multiplier=-1).then_inc(consts_made, 1)
            nc.gpsimd.iota(slot_row[:], pattern=[[1, K]], base=1, channel_multiplier=0,
                           allow_small_or_imprecise_dtypes=True).then_inc(consts_made, 1)
            nc.gpsimd.iota(token_row[:], pattern=[[1, S]], base=0, channel_multiplier=0,
                           allow_small_or_imprecise_dtypes=True).then_inc(consts_made, 1)
            nc.gpsimd.iota(row_i[:, 0:1], pattern=[[0, 1]], base=0, channel_multiplier=1).then_inc(consts_made, 1)
            nc.gpsimd.memset(zeros[:], 0.0).then_inc(consts_made, 1)
            nc.gpsimd.iota(facts[:, :, :, :, 0], pattern=[[0, C], [0, BE]], base=0, channel_multiplier=1,
                           allow_small_or_imprecise_dtypes=True).then_inc(consts_made, 1)
            nc.gpsimd.iota(facts[:, :, :, :, 1], pattern=[[P, C], [0, BE]], base=0, channel_multiplier=0,
                           allow_small_or_imprecise_dtypes=True).then_inc(consts_made, 1)

            def attention_constants():
                nc.gpsimd.memset(bias_row[:, 0:D], 0.0).then_inc(pool_consts, 1)
                nc.gpsimd.memset(v_ext[:], 0.0).then_inc(pool_consts, 1)
                pool.wait_ge(gate_up_done[0], 2 * MI * E)
                nc.gpsimd.memset(k_stack[:].bitcast(F32), 0.0).then_inc(pool_consts, 1)
                pool.wait_ge(pool_consts, 5)
                nc.gpsimd.memset(v_ext[:, :, :, :, DH + 1:DH + 2], 1.0).then_inc(attention_consts, 1)
                for jj in range(2):
                    pool.wait_ge(attention_consts, 1 + jj)
                    ones_rows = k_stack[64 * jj + 4 * DH:64 * jj + 4 * DH + 1].rearrange("r g (pp jj) t -> r g jj pp t", jj=2)[:, :, jj]
                    nc.gpsimd.memset(ones_rows.bitcast(F32), 1.0).then_inc(attention_consts, 1)

            def halves(l):
                for b in range(B):
                    t = slice(b * C, (b + 1) * C)
                    pool.wait_ge(xn_ready[2 * l], C * (b + 1))
                    nc.gpsimd.tensor_copy(xn_hi[:, t], xn[:, t]).then_inc(pool_halves[l], 1)
                    pool.wait_ge(pool_halves[l], b + 1)
                    nc.gpsimd.tensor_tensor(xn_lo[:, t], xn[:, t], xn_hi[:, t], ALU.subtract).then_inc(halves_ready[l], 1)

            def affinity_parts(l):
                parts = facts[:].rearrange("p (h cl) b e w -> p cl h (b e) w", cl=CL)
                aff = affinity[:].rearrange("p cl h b e -> p cl h (b e)")
                rest = residue[:].rearrange("p n cl h b e -> p n cl h (b e)")
                pool.wait_ge(affinity_ready[l], 1)
                sources = (aff, rest[:, 0], rest[:, 1])
                done = 0
                for n in range(3):
                    for cl in range(CL):
                        last = nc.gpsimd.tensor_copy(parts[:, cl, :, :, 2 + n], sources[n][:, cl])
                        last.then_inc(pool_facts[l] if n < 2 else facts_ready[l], 1)
                    if n < 2:
                        done += CL
                        pool.wait_ge(pool_facts[l], done)
                        for cl in range(CL):
                            nc.gpsimd.tensor_tensor(rest[:, n, cl], sources[n][:, cl], parts[:, cl, :, :, 2 + n], ALU.subtract).then_inc(pool_facts[l], 1)
                        done += CL
                        pool.wait_ge(pool_facts[l], done)

            def split_weights(l):
                def split(i, o):
                    u = o % 2
                    pool.wait_ge(w_hi_ready[l], after(i, o, 1, 1))
                    nc.gpsimd.tensor_tensor(w_lo[:, u].rearrange("p k i -> p (k i)"), w_gu[:, u].rearrange("p k i -> p (k i)"),
                                            w_hi[:, u].rearrange("p k i -> p (k i)").bitcast(F32), ALU.subtract).then_inc(w_lo_ready[l], 1)

                split(0, 0)
                split(0, 1)
                with pool.Fori(0, E // 2 - 1) as i:
                    for o in (2, 3):
                        split(i, o)

            halves(0)
            affinity_parts(0)
            split_weights(0)
            attention_constants()
            pool.wait_ge(attention_consts, 3)
            pool.wait_ge(gates_ready, 2)

            def extend_values(b):
                for g in range(G):
                    if not isinstance(b, int):
                        pool.wait_ge(probs_used, b * (C * G) + (C * (g - G) + 2 * C))
                    heads = slice(g * HG, (g + 1) * HG)
                    ex = expression[:, bass.ds(b * C, C), heads].unsqueeze(3)
                    v = vae[:, bass.ds(b * C, C), g * HG * DH:(g + 1) * HG * DH].rearrange("p c (j d) -> p c j d", d=DH)
                    nc.gpsimd.tensor_tensor(v_ext[:, g, :, :, 0:DH], v, ex.broadcast_to([P, C, HG, DH]), ALU.mult).then_inc(values_ready, 1)
                    nc.gpsimd.tensor_copy(v_ext[:, g, :, :, DH:DH + 1], ex).then_inc(values_ready, 1)

            extend_values(0)
            with pool.Fori(1, B) as b:
                extend_values(b)
            halves(1)
            affinity_parts(1)
            split_weights(1)

        @block.scalar
        def _(act):
            def root(n, b):
                t = slice(b * C, (b + 1) * C)
                act.wait_ge(var_ready[n], C * (b + 1))
                nc.scalar.activation(std[:, t], mean_var[:, t, 1], ACT.Sqrt, bias=norm_eps[:]).then_inc(std_ready[n], 1)

            def copy_xnT(n, b):
                act.wait_ge(xn_turned[n], b + 1)
                nc.scalar.copy(xnT[:, b, :], ps[:, b, :]).then_inc(xnT_ready[n], 1)

            def rotation():
                act.wait_ge(attn_weights_loaded, 16 * 12)
                nc.scalar.activation(hp[:, 0:3], head_params[:, 0:3], ACT.Exp, scale=-1.0).then_inc(act_rot, 1)
                nc.scalar.activation(hp[:, 3:4], head_params[:, 3:4], ACT.Tanh).then_inc(act_rot, 1)
                act.wait_ge(rot_ready, 1)
                nc.scalar.activation(hp[:, 10:12], hp[:, 8:10], ACT.Sin).then_inc(act_rot, 1)

            def round_weights(l, i, o):
                u = o % 2
                act.wait_ge(expert_loaded[l][u], 48 * i + 48 * (o // 2) + 48)
                if o > 1:
                    act.wait_ge(gate_up_done[l], after(i, o, 2 * MI, -2 * MI))
                nc.scalar.copy(w_hi[:, u].rearrange("p k i -> p (k i)"), w_gu[:, u].rearrange("p k i -> p (k i)")).then_inc(w_hi_ready[l], 1)

            def route(l):
                act.wait_ge(shifted_ready[l], 1)
                nc.scalar.activation(expo[:], shifted[:], ACT.Exp).then_inc(exp_ready[l], 1)
                if l == 0:
                    rotation()
                round_weights(l, 0, 0)
                round_weights(l, 0, 1)
                for n in range(2 * B):
                    b, first = n // 2, 4 * (n % 2)
                    act.wait_ge(gathered[l], n + 1)
                    for k, picked in enumerate((picked_hi, picked_lo)):
                        nc.scalar.copy(picked[:, first:first + 4, b, :],
                                       ps[:, pick_bank(n) + k, :].rearrange("p (e s) -> p e s", e=4)).then_inc(picked_ready[l], 1)

            def experts(l):
                def silus(i, o):
                    for m in range(MI):
                        act.wait_ge(gate_up_done[l], after(i, o, 2 * MI, 2 * m + 1))
                        act.wait_ge(hidden_ready[l], after(i, o, MI, m + 1))
                        nc.scalar.activation(silu[:, m, :], ps[:, 4 + 2 * m, :], ACT.Silu).then_inc(silu_ready[l], 1)

                def copy_down(i, o):
                    act.wait_ge(down_done[l], after(i, o, 1, 1))
                    nc.scalar.copy(down_out[:], ps[:, 6, :]).then_inc(down_copied[l], 1)

                silus(0, 0)
                with act.Fori(0, E // 2 - 1) as i:
                    for o in (1, 2):
                        copy_down(i, o - 1)
                        silus(i, o)
                        round_weights(l, i, o + 1)
                copy_down(0, E - 2)
                silus(0, E - 1)
                copy_down(0, E - 1)
                for b in range(B):
                    act.wait_ge(scattered[l], b + 1)
                    nc.scalar.mul(moeT[:, b, :], ps[:, b, :], 0.5).then_inc(moeT_ready[l], 1)

            act.wait_ge(eps_made, 1)
            root(0, 0)
            for b in range(B):
                if b < B - 1:
                    root(0, b + 1)
                copy_xnT(0, b)
            route(0)
            experts(0)

            def copy_qk_hi(b):
                for qk in range(2):
                    act.wait_ge(qk_projected, 2 * b + qk + 1)
                    if b >= 2:
                        act.wait_ge(hi_stored[b % 2][qk], 16 * (b // 2))
                    nc.scalar.copy(part_hi[:, b % 2, qk, :], ps[:, 4 + qk, :]).then_inc(qk_hi_ready, 1)

            def copy_max_rows(n, slot):
                act.wait_ge(max_turned, n + 1)
                nc.scalar.copy(max_rows[:, slot, :], ps[0:HG, 7, :]).then_inc(max_rows_ready, 1)

            root(1, 0)
            copy_xnT(1, 0)
            root(1, 1)
            copy_qk_hi(0)
            root(1, 2)
            copy_xnT(1, 1)
            copy_xnT(1, 2)
            root(1, 3)
            copy_qk_hi(1)
            copy_xnT(1, 3)
            copy_qk_hi(2)
            copy_qk_hi(3)
            copy_max_rows(0, 0)
            act.wait_ge(vae_ready, T // 2)
            nc.scalar.activation(gate_exp, vae[:, :, D:], ACT.Exp, scale=-1.0).then_inc(gate_exp_ready, 1)

            def copy_heads(n, slot):
                act.wait_ge(probs_used, n * C + 2 * C)
                act.wait_ge(heads_turned, n + 1)
                nc.scalar.copy(heads_out[:, slot, :], ps[:, 6, :]).then_inc(heads_copied, 1)

            def attend(b, step, has_before, has_next):
                n, g = b * G + step, step % G
                for u in range(EXP_UNITS):
                    act.wait_ge(scores_ready, n * EXP_UNITS + (u + 2))
                    if u % HG == 0:
                        act.wait_ge(probs_used, n * C + (u // HG + 1))
                    nc.scalar.activation(probs[:, u // HG, u % HG, :], ps[:, RING + ring_bank(step, u), :],
                                         ACT.Exp, scale=SCORE_SCALE).then_inc(probs_ready, 1)
                    if u == 2 and has_next:
                        copy_max_rows(n + 1, (g + 1) % 2)
                    if u == HEADS_AT and has_before:
                        copy_heads(n - 1, (g - 1) % 2)

            attend(0, 0, False, True)
            with act.Fori(0, B - 1) as b:
                for step in range(1, G + 1):
                    attend(b, step, True, True)
            for step in range(1, G):
                attend(B - 1, step, True, step < G - 1)
            for b in range(B - 1):
                root(2, b)
            copy_heads(B * G - 1, 1)
            copy_xnT(2, 0)
            copy_xnT(2, 1)
            root(2, B - 1)
            copy_xnT(2, 2)
            copy_xnT(2, 3)
            route(1)
            experts(1)

        @block.vector
        def _(dve):
            def norm_stats(n, b, steps):
                tiles = range(b * C, (b + 1) * C)
                for t in tiles:
                    steps.did(nc.vector.bn_stats(out=stats[:, t, :], in_=x[:, t, :]))
                steps.settle()
                for t in tiles:
                    nc.vector.bn_aggr(out=mean_var[:, t, :], in_=stats[:, t, :]).then_inc(var_ready[n], 1)

            def norm_apply(n, b, steps):
                t0 = slice(b * C, (b + 1) * C)
                dve.wait_ge(std_ready[n], b + 1)
                steps.did(nc.vector.reciprocal(rstd[:, t0], std[:, t0]))
                steps.settle()
                for t in range(b * C, (b + 1) * C):
                    nc.vector.tensor_scalar(xn[:, t, :], x[:, t, :], mean_var[:, t, 0:1], rstd[:, t:t + 1],
                                            ALU.subtract, ALU.mult).then_inc(xn_ready[n], 1)

            def rotation_angles(steps):
                dve.wait_ge(ident_made, 1)
                dve.wait_ge(consts_made, 7)
                swapped = swap_rows[:].rearrange("p (h s q) -> p h s q", s=2, q=DH // 2)
                straight = ident[:].rearrange("p (h s q) -> p h s q", s=2, q=DH // 2)
                for s in range(2):
                    nc.vector.tensor_copy(swapped[:, :, s], straight[:, :, 1 - s]).then_inc(swap_ready, 1)
                steps.did(nc.vector.tensor_scalar(row_i[:, 1:2], row_i[:, 0:1], 4, None, ALU.bitwise_and))
                dve.wait_ge(act_rot, 2)
                steps.did(nc.vector.tensor_scalar(hp[:, 0:3], hp[:, 0:3], 1.0, None, ALU.add))
                steps.settle()
                steps.did(nc.vector.tensor_scalar(hp[:, 15:16], row_i[:, 1:2], -0.5, 1.0, ALU.mult, ALU.add))
                steps.did(nc.vector.reciprocal(hp[:, 4:7], hp[:, 0:3]))
                steps.settle()
                steps.did(nc.vector.tensor_scalar(hp[:, 8:9], hp[:, 4:5], -math.pi, math.pi / 2, ALU.mult, ALU.add))
                steps.settle()
                steps.did(nc.vector.scalar_tensor_tensor(out=hp[:, 7:8], in0=hp[:, 8:9], scalar=-1.0, in1=hp[:, 8:9],
                                                         op0=ALU.mult, op1=ALU.min))
                steps.settle()
                nc.vector.tensor_scalar(hp[:, 9:10], hp[:, 7:8], math.pi / 2, None, ALU.add).then_inc(rot_ready, 1)

            def rotation_rows(steps):
                steps.did(nc.vector.tensor_tensor(hp[:, 12:13], hp[:, 5:6], hp[:, 6:7], ALU.mult))
                steps.settle()
                steps.did(nc.vector.tensor_tensor(hp[:, 12:13], hp[:, 12:13], hp[:, 3:4], ALU.mult))
                steps.settle()
                dve.wait_ge(act_rot, 3)
                steps.did(nc.vector.tensor_tensor(hp[:, 13:14], hp[:, 12:13], hp[:, 10:11], ALU.mult))
                steps.did(nc.vector.tensor_tensor(hp[:, 14:15], hp[:, 12:13], hp[:, 11:12], ALU.mult))
                steps.settle()
                steps.did(nc.vector.tensor_tensor(hp[:, 14:15], hp[:, 14:15], hp[:, 15:16], ALU.mult))
                steps.did(nc.vector.tensor_scalar(w_rot[:], wout_sb[:], hp[:, 13:14], None, ALU.mult))
                steps.settle()
                dve.wait_ge(wout_swapped, 1)
                nc.vector.scalar_tensor_tensor(out=w_rot[:], in0=ps[:, 7, 0:D], scalar=hp[:, 14:15], in1=w_rot[:],
                                               op0=ALU.mult, op1=ALU.add).then_inc(rot_ready, 1)

            def route(l):
                steps = Steps(dve, dve_route[l])
                logits = ps[:, 4, 0:T * E].rearrange("p (t e) -> p t e", e=E)
                sh, ex, af = (a[:].rearrange("p cl h b e -> p (cl h b) e") for a in (shifted, expo, affinity))
                dve.wait_ge(logits_ready[l], B)
                steps.did(nc.vector.tensor_reduce(top[:], logits, AX.X, ALU.max))
                steps.settle()
                nc.vector.tensor_tensor(sh, logits, top[:].unsqueeze(2).broadcast_to([P, T, E]), ALU.subtract).then_inc(shifted_ready[l], 1)
                dve.wait_ge(exp_ready[l], 1)
                steps.did(nc.vector.tensor_reduce(total[:], ex, AX.X, ALU.add))
                steps.settle()
                steps.did(nc.vector.reciprocal(rtotal[:], total[:]))
                steps.settle()
                nc.vector.tensor_tensor(af, ex, rtotal[:].unsqueeze(2).broadcast_to([P, T, E]), ALU.mult).then_inc(affinity_ready[l], 1)
                if l == 0:
                    rot_steps = Steps(dve, dve_rot)
                    rotation_angles(rot_steps)
                dve.wait_ge(affinity_turned[l], 1)
                steps.did(nc.vector.tensor_copy(work[:, 0, :], ps[0:2 * BE, 5, 0:S // 2]))
                steps.settle()
                for r in range(K // 8):
                    now, then, eight = work[:, r % 2, :], work[:, (r + 1) % 2, :], slice(8 * r, 8 * r + 8)
                    steps.did(nc.vector.max(out=values[:, eight], in_=now))
                    steps.settle()
                    if r < K // 8 - 1:
                        steps.did(nc.vector.match_replace(out=then, in_to_replace=values[:, eight], in_values=now, imm_value=LOWEST))
                        steps.settle()
                steps.did(nc.vector.tensor_copy(flipped[:], values[BE:2 * BE, ::-1]))
                steps.settle()
                steps.did(nc.vector.tensor_tensor(flipped[:], flipped[:], values[0:BE, :], ALU.max))
                steps.settle()
                steps.did(nc.vector.tensor_reduce(threshold[:], flipped[:], AX.X, ALU.min))
                steps.settle()
                nc.vector.tensor_copy(threshold_row[:], threshold[:].broadcast_to([BE, P])).then_inc(threshold_ready[l], 1)
                if l == 0:
                    rotation_rows(rot_steps)
                dve.wait_ge(threshold_turned[l], 1)
                aff = affinity[:].rearrange("p cl h b e -> p cl h (b e)")
                for kind, op in enumerate((ALU.is_gt, ALU.is_equal)):
                    for h in range(2):
                        nc.vector.tensor_tensor(marks[:, kind, CL * h:CL * h + CL], aff[:, :, h],
                                                ps[:, 6, 0:BE].unsqueeze(1).broadcast_to([P, CL, BE]), op).then_inc(marks_ready[l], 1)
                dve.wait_ge(marks_counted[l], 1)
                before = ps[:, 0, 0:2 * (C + 1) * BE].rearrange("p (k c r) -> p k c r", k=2, c=C + 1)
                left = equals_left[:].unsqueeze(1).broadcast_to([P, C, BE])
                steps.did(nc.vector.tensor_scalar(equals_left[:], before[:, 0, C], -1.0, float(K), ALU.mult, ALU.add))
                steps.settle()
                steps.did(nc.vector.tensor_tensor(equal_taken[:], before[:, 1, 0:C], left, ALU.is_lt))
                steps.did(nc.vector.tensor_tensor(equals_before[:], before[:, 1, 0:C], left, ALU.min))
                steps.settle()
                steps.did(nc.vector.tensor_tensor(equal_taken[:], equal_taken[:], marks[:, 1], ALU.mult))
                steps.did(nc.vector.tensor_tensor(slot_before[:], before[:, 0, 0:C], equals_before[:], ALU.add))
                steps.settle()
                steps.did(nc.vector.tensor_tensor(taken[:], equal_taken[:], marks[:, 0], ALU.add))
                steps.settle()
                nc.vector.scalar_tensor_tensor(out=slot[:], in0=slot_before[:], scalar=1.0, in1=taken[:],
                                               op0=ALU.add, op1=ALU.mult).then_inc(slot_ready[l], 1)
                dve.wait_ge(slot_ready[l], 1)
                for b in range(B):
                    for c in range(C):
                        nc.vector.tensor_tensor(pick[:, b, c], slot_row[:].unsqueeze(1).broadcast_to([P, E, K]),
                                                slot[:, c, b * E:(b + 1) * E].unsqueeze(2).broadcast_to([P, E, K]),
                                                ALU.is_equal).then_inc(pick_ready[l], 1)
                dve.wait_ge(facts_gathered[l], 1)
                facts_by_slot = ps[:, 1, 0:5 * BE].rearrange("p (r w) -> p r w", w=5)
                nc.vector.tensor_reduce(indexT[:].rearrange("p b e -> p (b e)"), facts_by_slot[:, :, 0:2], AX.X, ALU.add).then_inc(slot_facts_ready[l], 1)
                nc.vector.tensor_reduce(gateT[:].rearrange("p b e -> p (b e)"), facts_by_slot[:, :, 2:5], AX.X, ALU.add).then_inc(slot_facts_ready[l], 1)

            def experts(l):
                def make_place(i, o):
                    u = o % 2
                    dve.wait_ge(scatter_done[l], after(i, o, 1, 1))
                    for b in range(B):
                        nc.vector.tensor_scalar(place[:, u, b, :], token_row[:], indexT[:, b, bass.ds(2 * i + o, 1)], None,
                                                ALU.is_equal).then_inc(place_ready[l], 1)

                def gate_times_up(i, o):
                    u = o % 2
                    for m in range(MI):
                        dve.wait_ge(silu_ready[l], after(i, o, MI, m + 1))
                        dve.wait_ge(gate_up_done[l], after(i, o, 2 * MI, 2 * m + 2))
                        nc.vector.tensor_tensor(hidden[:, u, m, :], silu[:, m, :], ps[:, 5 - m, :], ALU.mult).then_inc(hidden_ready[l], 1)

                def weigh(i, o, before=True):
                    u = o % 2
                    dve.wait_ge(down_turned[l], after(i, o, 1, 1))
                    if before:
                        dve.wait_ge(scatter_ready[l], after(i, o, 2))
                    nc.vector.tensor_tensor(weighted[:], ps[:, 7, :].rearrange("p (b d) -> p b d", b=B),
                                            gateT[:, :, bass.ds(2 * i + o, 1)].broadcast_to([P, B, D]), ALU.mult).then_inc(weighted_ready[l], 1)
                    dve.wait_ge(weighted_ready[l], after(i, o, 1, 2))
                    dve.wait_ge(scatter_done[l], after(i, o, 1, 1))
                    nc.vector.tensor_copy(wy_hi[:, u], weighted[:]).then_inc(scatter_ready[l], 1)
                    dve.wait_ge(scatter_ready[l], after(i, o, 2, 1))
                    nc.vector.tensor_tensor(wy_lo[:, u], weighted[:], wy_hi[:, u].bitcast(F32), ALU.subtract).then_inc(scatter_ready[l], 1)

                gate_times_up(0, 0)
                dve.wait_ge(slot_facts_ready[l], 2)
                make_place(0, 0)
                gate_times_up(0, 1)
                weigh(0, 0, before=False)
                make_place(0, 1)
                with dve.Fori(0, E // 2 - 1) as i:
                    for o in (2, 3):
                        gate_times_up(i, o)
                        weigh(i, o - 1)
                        make_place(i, o)
                weigh(0, E - 1)

            def add_moe(l, b):
                dve.wait_ge(moe_turned[l], b + 1)
                xs = x[:, b * C:(b + 1) * C, :].rearrange("p c d -> p (c d)")
                nc.vector.tensor_tensor(xs, xs, ps[:, 4 + b, :], ALU.add).then_inc(x_added[l], 1)

            def take_max(n, step, u):
                g = step % G
                col, qt = u // C, u % C
                dve.wait_ge(max_scores_ready, n * MAX_UNITS + (u + 1))
                nc.vector.tensor_reduce(neg_max[:, g, qt, col:col + 1], ps[:, ring_bank(step, u), :], AX.X, ALU.max, negate=True).then_inc(max_taken, 1)

            def take_maxima(n, units):
                for u in units:
                    take_max(n, n, u)

            steps = Steps(dve, dve_norm[0])
            for b in range(B):
                dve.wait_ge(x_loaded[b], 16)
                norm_stats(0, b, steps)
                if b > 0:
                    norm_apply(0, b - 1, steps)
            norm_apply(0, B - 1, steps)
            route(0)
            experts(0)

            def split_qk_lo(b):
                for qk in range(2):
                    dve.wait_ge(qk_hi_ready, 2 * b + qk + 1)
                    if b >= 2:
                        dve.wait_ge(lo_stored[b % 2][qk], 16 * (b // 2))
                    nc.vector.tensor_tensor(part_lo[:, b % 2, qk, :], ps[:, 4 + qk, :], part_hi[:, b % 2, qk, :].bitcast(F32),
                                            ALU.subtract).then_inc(qk_lo_ready, 1)

            def add_bias(b):
                for w in range(2):
                    n = 2 * b + w
                    dve.wait_ge(vae_projected, n + 1)
                    nc.vector.tensor_tensor(vae[:, 2 * n:2 * n + 2, :], ps[:, 6 + w, 0:2 * (D + 2 * H)].rearrange("p (t f) -> p t f", t=2),
                                            bias_row[:].unsqueeze(1).broadcast_to([P, 2, D + 2 * H]), ALU.add).then_inc(vae_ready, 1)

            steps = Steps(dve, dve_norm[1])
            add_moe(0, 0)
            for b in range(B):
                dve.wait_ge(x_added[0], b + 1)
                norm_stats(1, b, steps)
                if b < B - 1:
                    add_moe(0, b + 1)
                    norm_apply(1, b, steps)
                if b == B - 2:
                    split_qk_lo(0)
            norm_apply(1, B - 1, steps)
            dve.wait_ge(attention_consts, 3)
            add_bias(0)
            split_qk_lo(1)
            add_bias(1)
            split_qk_lo(2)
            add_bias(2)
            take_maxima(0, range(MAX_UNITS))
            split_qk_lo(3)
            take_maxima(1, range(MAX_UNITS // 2))
            add_bias(3)
            take_maxima(1, range(MAX_UNITS // 2, MAX_UNITS))
            dve.wait_ge(gate_exp_ready, 1)
            nc.vector.tensor_scalar(gate_one, gate_exp, 1.0, None, ALU.add).then_inc(gate_one_ready, 1)
            dve.wait_ge(gate_one_ready, 1)
            nc.vector.reciprocal(expression[:], gate_one[:, :, H:]).then_inc(gates_ready, 1)
            nc.vector.tensor_scalar(z_weight[:], gate_one[:, :, 0:H], SUM_EPS, None, ALU.mult).then_inc(gates_ready, 1)
            dve.wait_ge(gates_ready, 2)

            def norm_heads(b, g, steps, between=lambda: None):
                n = b * G + g
                dve.wait_ge(heads_turned, n + 3)
                o = ps[:, 7, :].rearrange("p (c j w) -> p c j w", c=C, j=HG)
                zw = z_weight[:, bass.ds(b * C, C), g * HG:(g + 1) * HG]
                steps.did(nc.vector.tensor_tensor(den_a[:], o[:, :, :, DH + 1], zw, ALU.mult))
                between()
                steps.settle()
                steps.did(nc.vector.tensor_tensor(den_b[:], o[:, :, :, DH], den_a[:], ALU.add))
                between()
                steps.settle()
                steps.did(nc.vector.reciprocal(den_r[:], den_b[:]))
                between()
                steps.settle()
                dst = combined[:, bass.ds(b * C, C), g * HG * DH:(g + 1) * HG * DH].rearrange("p c (j d) -> p c j d", j=HG)
                nc.vector.tensor_tensor(dst, o[:, :, :, 0:DH], den_r[:].unsqueeze(3).broadcast_to([P, C, HG, DH]),
                                        ALU.mult).then_inc(heads_normed, 1)

            def attend(b, step, steps, has_max):
                n = b * G + step
                units = iter(range(MAX_UNITS) if has_max else ())

                def take(count):
                    for _ in range(count):
                        u = next(units, None)
                        if u is not None:
                            take_max(n + 2, step + 2, u)

                take(NORM_AT)
                if step > 0:
                    norm_heads(b, step - 1, steps, lambda: take(1))
                take(MAX_UNITS)

            attend(0, 0, None, True)
            with dve.Fori(0, B - 1) as b:
                steps = Steps(dve, dve_heads, b, 3 * G)
                for step in range(1, G + 1):
                    attend(b, step, steps, True)
                steps.end_turn()

            def copy_combined(b):
                dve.wait_ge(combined_turned, b + 1)
                nc.vector.tensor_copy(combinedT[:, b, :], ps[:, TURN_BANK[b], :]).then_inc(combinedT_ready, 1)

            def add_attention(b):
                dve.wait_ge(attention_out, b + 1)
                xs = x[:, b * C:(b + 1) * C, :].rearrange("p c d -> p (c d)")
                nc.vector.tensor_tensor(xs, xs, ps[:, OUT_BANK[b], :], ALU.add).then_inc(x_attended, 1)
                dve.wait_ge(x_attended, b + 1)
                norm_stats(2, b, norm_steps)

            steps = Steps(dve, dve_heads, B - 1, 3 * G)
            norm_steps = Steps(dve, dve_norm[2])
            attend(B - 1, 1, steps, True)
            copy_combined(0)
            add_attention(0)
            copy_combined(1)
            norm_heads(B - 1, 1, steps)
            add_attention(1)
            copy_combined(2)
            add_attention(2)
            norm_heads(B - 1, 2, steps)
            norm_apply(2, 0, norm_steps)
            norm_heads(B - 1, 3, steps)
            copy_combined(3)
            norm_apply(2, 1, norm_steps)
            add_attention(3)
            norm_apply(2, 2, norm_steps)
            norm_apply(2, 3, norm_steps)
            route(1)
            experts(1)
            for b in range(B):
                add_moe(1, b)

        @block.tensor
        def _(pe):
            def chunk(c):
                return slice(c * P, (c + 1) * P)

            def turn_xn(n, b):
                for c in range(C):
                    pe.wait_ge(xn_ready[n], C * b + c + 1)
                    last = nc.tensor.transpose(ps[:, b, chunk(c)], xn[:, C * b + c, :], ident[:])
                last.then_inc(xn_turned[n], 1)

            def logits(l, b):
                pe.wait_ge(xnT_ready[2 * l], b + 1)
                for c in range(C):
                    col = ((c % CL * 2 + c // CL) * B + b) * E
                    last = nc.tensor.matmul(ps[:, 4, col:col + E], xnT[:, b, chunk(c)], gate_sb[:], start=True, stop=True)
                last.then_inc(logits_ready[l], 1)

            def route(l):
                pe.wait_ge(affinity_ready[l], 1)
                for cl in range(CL):
                    last = nc.tensor.transpose(ps[0:2 * BE, 5, chunk(cl)], affinity[:, cl].rearrange("p h b e -> p (h b e)"), ident[:])
                last.then_inc(affinity_turned[l], 1)
                if l == 0:
                    pe.wait_ge(swap_ready, 2)
                    pe.wait_ge(attn_weights_loaded, 16 * 12)
                    nc.tensor.matmul(ps[:, 7, 0:D], swap_rows[:], wout_sb[:], start=True, stop=True).then_inc(wout_swapped, 1)
                pe.wait_ge(threshold_ready[l], 1)
                nc.tensor.transpose(ps[:, 6, 0:BE], threshold_row[:], ident[0:BE, 0:BE]).then_inc(threshold_turned[l], 1)
                pe.wait_ge(consts_made, 7)
                pe.wait_ge(marks_ready[l], 4)
                before = ps[:, 0, 0:2 * (C + 1) * BE].rearrange("p (k c r) -> p k c r", k=2, c=C + 1)
                nc.tensor.matmul(before[:, :, 0:1], earlier[:], marks[:, :, 0:1], start=True, stop=True, skip_group_check=True)
                nc.tensor.matmul(before[:, :, 1:C + 1], ones[:], marks[:], start=True, stop=False, skip_group_check=True)
                nc.tensor.matmul(before[:, :, 1:C], earlier[:], marks[:, :, 1:C], start=False, stop=False, skip_group_check=True)
                for lag in range(2, C + 1):
                    last = nc.tensor.matmul(before[:, :, lag:C + 1], ones[:], marks[:, :, 0:C + 1 - lag], start=False, stop=lag == C, skip_group_check=True)
                last.then_inc(marks_counted[l], 1)
                if l == 0:
                    pe.wait_ge(rot_ready, 2)
                for b in range(B):
                    pe.wait_ge(halves_ready[l], b + 1)
                    if b == 0:
                        pe.wait_ge(facts_ready[l], CL)
                    for hf in range(2):
                        n = 2 * b + hf
                        if n >= 3:
                            pe.wait_ge(picked_ready[l], 2 * (n - 2))
                        for c in range(C):
                            pe.wait_ge(pick_ready[l], C * b + c + 1)
                            for k, half in enumerate((xn_hi, xn_lo)):
                                last = nc.tensor.matmul(ps[:, pick_bank(n) + k, :], half[:, C * b + c, :], pick[:, b, c, 4 * hf:4 * hf + 4, :],
                                                        start=(c == 0), stop=(c == C - 1))
                        last.then_inc(gathered[l], 1)
                    for e in range(E):
                        col = 5 * (b * E + e)
                        for c in range(C):
                            last = nc.tensor.matmul(ps[:, 1, col:col + 5], pick[:, b, c, e, :], facts[:, c, b, e, :], start=(c == 0), stop=(c == C - 1))
                last.then_inc(facts_gathered[l], 1)

            def experts(l):
                pe.wait_ge(picked_ready[l], 4 * B)
                def gate_up(i, o):
                    u = o % 2
                    pe.wait_ge(w_lo_ready[l], after(i, o, 1, 1))
                    tokens_hi, tokens_lo = (a[:, bass.ds(2 * i + o, 1)].rearrange("p e b s -> p (e b s)") for a in (picked_hi, picked_lo))

                    def product(bank, k, cols):
                        nc.tensor.matmul(ps[:, bank, :], w_hi[:, u, k, cols], tokens_hi, start=True, stop=False)
                        nc.tensor.matmul(ps[:, bank, :], w_hi[:, u, k, cols], tokens_lo, start=False, stop=False)
                        nc.tensor.matmul(ps[:, bank, :], w_lo[:, u, k, cols], tokens_hi, start=False, stop=True).then_inc(gate_up_done[l], 1)

                    for m in range(MI):
                        cols = slice(m * P, (m + 1) * P)
                        if m == 1 and o > 0:
                            pe.wait_ge(down_copied[l], after(i, o, 1))
                        product(4 + 2 * m, 0, cols)
                        if m == 1:
                            pe.wait_ge(silu_ready[l], after(i, o, MI, 1))
                        product(5 - m, 1, cols)

                def down(i, o):
                    u = o % 2
                    pe.wait_ge(hidden_ready[l], after(i, o, MI, 2 * MI))
                    for m in range(MI):
                        last = nc.tensor.matmul(ps[:, 6, :], wd_sb[:, u, m, :], hidden[:, u, m, :], start=(m == 0), stop=(m == MI - 1))
                    last.then_inc(down_done[l], 1)

                def turn_down(i, o):
                    pe.wait_ge(down_copied[l], after(i, o, 1, 1))
                    pe.wait_ge(weighted_ready[l], after(i, o, 1, 1))
                    for b in range(B):
                        last = nc.tensor.transpose(ps[:, 7, chunk(b)], down_out[:, chunk(b)], ident[:])
                    last.then_inc(down_turned[l], 1)

                def scatter(i, o, final):
                    u = o % 2
                    pe.wait_ge(place_ready[l], after(i, o, B, B))
                    pe.wait_ge(scatter_ready[l], after(i, o, 2, 2))
                    for b in range(B):
                        nc.tensor.matmul(ps[:, b, :], wy_hi[:, u, b, :], place[:, u, b, :], start=False, stop=False, skip_group_check=True)
                        last = nc.tensor.matmul(ps[:, b, :], wy_lo[:, u, b, :], place[:, u, b, :], start=False, stop=final, skip_group_check=True)
                        if final:
                            last.then_inc(scattered[l], 1)
                    if not final:
                        last.then_inc(scatter_done[l], 1)

                gate_up(0, 0)
                pe.wait_ge(slot_facts_ready[l], 2)
                for b in range(B):
                    nc.tensor.matmul(ps[:, b, :], zeros[:, 0:P], zeros[:], start=True, stop=True)
                down(0, 0)
                gate_up(0, 1)
                turn_down(0, 0)
                with pe.Fori(0, E // 2 - 1) as i:
                    for o in (1, 2):
                        down(i, o)
                        gate_up(i, o + 1)
                        turn_down(i, o)
                        scatter(i, o - 1, False)
                down(0, E - 1)
                turn_down(0, E - 1)
                scatter(0, E - 2, False)
                scatter(0, E - 1, True)
                pe.wait_ge(weighted_ready[l], E + 1)
                for b in range(B):
                    pe.wait_ge(moeT_ready[l], b + 1)
                    for c in range(C):
                        last = nc.tensor.transpose(ps[:, 4 + b, chunk(c)], moeT[:, b, chunk(c)], ident[:])
                    last.then_inc(moe_turned[l], 1)

            pe.wait_ge(ident_made, 1)
            turn_xn(0, 0)
            pe.wait_ge(gate_loaded, 16)
            for b in range(1, B):
                turn_xn(0, b)
                logits(0, b - 1)
            logits(0, B - 1)
            route(0)
            experts(0)

            def project_qk(b):
                pe.wait_ge(xnT_ready[1], b + 1)
                if b == 0:
                    pe.wait_ge(x_added[0], 2)
                for qk, w in enumerate((wi_sb, wo_sb)):
                    if b > 0:
                        pe.wait_ge(qk_lo_ready, 2 * (b - 1) + qk + 1)
                    nc.tensor.matmul(ps[:, 4 + qk, :], w[:], xnT[:, b, :], start=True, stop=True).then_inc(qk_projected, 1)

            def project_vae(b):
                pe.wait_ge(xnT_ready[1], b + 1)
                if b == 0:
                    pe.wait_ge(x_added[0], B)
                for w in range(2):
                    if b > 0:
                        pe.wait_ge(vae_ready, 2 * (b - 1) + w + 1)
                    if b == 3 and w == 1:
                        pe.wait_ge(max_rows_ready, 1)
                    for c in range(2):
                        f = slice(c * (D + 2 * H), (c + 1) * (D + 2 * H))
                        last = nc.tensor.matmul(ps[:, 6 + w, f], xnT[:, b, chunk(2 * w + c)], wvae_sb[:], start=True, stop=True)
                    last.then_inc(vae_projected, 1)

            turn_xn(1, 0)
            project_qk(0)
            turn_xn(1, 1)
            turn_xn(1, 2)
            project_vae(0)
            project_qk(1)
            project_vae(1)
            turn_xn(1, 3)
            project_qk(2)
            project_vae(2)

            def max_scores(n, step, u):
                g, qt = step % G, u % C
                jj, pp = u // C // 2, u // C % 2
                pe.wait_ge(max_taken, ring_wait(n, step, u, 3))
                nc.tensor.matmul(ps[:, ring_bank(step, u), :], q_stack[:, g, pp, chunk(qt)], k_stack[:, g, 2 * pp + jj, :],
                                 start=True, stop=True).then_inc(max_scores_ready, 1)

            def turn_max(n, g, normed):
                pe.wait_ge(max_taken, n * MAX_UNITS + (MAX_UNITS + RING))
                if normed is not None:
                    pe.wait_ge(heads_normed, normed)
                for qt in range(C):
                    last = nc.tensor.transpose(ps[0:HG, 7, chunk(qt)], neg_max[:, g, qt, :], ident[:])
                last.then_inc(max_turned, 1)

            def scores(n, step, u):
                g, c, j = step % G, u // HG, u % HG
                pe.wait_ge(probs_ready, ring_wait(n, step, u, 1))
                nc.tensor.matmul(ps[:, RING + ring_bank(step, u), :], k_stack[:, g, j, chunk(c)], q_stack[:, g, j // 2, :],
                                 start=True, stop=True).then_inc(scores_ready, 1)

            def products(n, g, c):
                pe.wait_ge(probs_ready, n * EXP_UNITS + (HG * c + HG + RING))
                if c == 0:
                    pe.wait_ge(values_ready, 2 * n + 2)
                    pe.wait_ge(heads_copied, n + 1)
                for j in range(HG):
                    last = nc.tensor.matmul(ps[32 * j:32 * j + 32, 6, :], v_ext[:, g, c, j, :], probs[:, c, j, :],
                                            start=(c == 0), stop=(c == C - 1))
                last.then_inc(probs_used, 1)

            def turn_heads(n, g, rows):
                pe.wait_ge(heads_copied, n + 2)
                pe.wait_ge(max_rows_ready, rows)
                pe.wait_ge(heads_normed, n + 1)
                for qt in range(C):
                    last = nc.tensor.transpose(ps[:, 7, chunk(qt)], heads_out[:, g % 2, chunk(qt)], ident[:])
                last.then_inc(heads_turned, 1)

            def attend(b, step, first=False, last_batch=False):
                g, n = step % G, b * G + step
                pe.wait_ge(max_rows_loaded[g], (b + step // G) * 32 + 32)
                has_max = not last_batch or step < 2
                if has_max:
                    pe.wait_ge(stacks_loaded[(g + 2) % G], (b + (step + 2) // G) * 96 + 96)
                has_next = not last_batch or step < G - 1
                for k in range(MAX_UNITS // 2):
                    scores(n, step, 2 * k)
                    if has_max:
                        max_scores(n + 2, step + 2, 2 * k)
                    scores(n, step, 2 * k + 1)
                    if k == 0 and has_next:
                        turn_max(n + 1, (g + 1) % G, None if first else n)
                    if last_batch and step > 1:
                        done = 2 * (step - 2) + k // 4
                        if k % 4 == 0 and done < B - 1:
                            turn_combined(done)
                        if k % 4 == 2 and done < B - 1:
                            project_out(done)
                    if k == 1 and not first:
                        products(n - 1, (g - 1) % G, C - 1)
                    if k in (3, 5, 7):
                        products(n, g, k // 2 - 1)
                    if not first and k == TURN_AT:
                        turn_heads(n - 1, g - 1, n + (2 if has_next else 1))
                    if has_max:
                        max_scores(n + 2, step + 2, 2 * k + 1)

            def first_maxima(n, units):
                pe.wait_ge(stacks_loaded[n], 96)
                for u in units:
                    max_scores(n, n, u)

            pe.wait_ge(xnT_ready[1], B)
            first_maxima(0, range(RING))
            project_qk(3)
            first_maxima(0, range(RING, MAX_UNITS))
            pe.wait_ge(vae_ready, 2 * 3)
            turn_max(0, 0, None)
            first_maxima(1, range(MAX_UNITS // 2))
            project_vae(3)
            first_maxima(1, range(MAX_UNITS // 2, MAX_UNITS))
            pe.wait_ge(vae_ready, 2 * B)
            pe.wait_ge(qk_lo_ready, 2 * B)
            attend(0, 0, first=True)
            with pe.Fori(0, B - 1) as b:
                for step in range(1, G + 1):
                    attend(b, step)

            def turn_combined(b):
                pe.wait_ge(heads_normed, G * (b + 1) + 1)
                if 0 < b < B - 1:
                    pe.wait_ge(combinedT_ready, b)
                for c in range(C):
                    last = nc.tensor.transpose(ps[:, TURN_BANK[b], chunk(c)], combined[:, C * b + c, :], ident[:])
                last.then_inc(combined_turned, 1)

            def project_out(b):
                pe.wait_ge(combinedT_ready, b + 1)
                if 0 < b < B - 1:
                    pe.wait_ge(x_attended, b)
                for c in range(C):
                    last = nc.tensor.matmul(ps[:, OUT_BANK[b], chunk(c)], combinedT[:, b, chunk(c)], w_rot[:], start=True, stop=True)
                last.then_inc(attention_out, 1)

            for step in range(1, G):
                attend(B - 1, step, last_batch=True)
            products(B * G - 1, G - 1, C - 1)
            turn_heads(B * G - 1, G - 1, B * G)
            turn_xn(2, 0)
            turn_combined(3)
            project_out(3)
            turn_xn(2, 1)
            pe.wait_ge(x_attended, B)
            logits(1, 0)
            turn_xn(2, 2)
            logits(1, 1)
            turn_xn(2, 3)
            logits(1, 2)
            logits(1, 3)

            route(1)
            experts(1)


_INS = ["L0_attn_x", "L0_attn_Wa", "L0_attn_ba", "L0_attn_We", "L0_attn_be", "L0_attn_Wi", "L0_attn_Wo", "L0_attn_Wv",
        "L0_attn_Wout", "L0_attn_chi", "L0_attn_beta_p", "L0_attn_iv_p", "L0_attn_ov_p", "L0_ffn_gate_w", "L0_ffn_Wg",
        "L0_ffn_Wu", "L0_ffn_Wd"]
_OUTS = [((4, 512, 128), "float32")]


def kernel(**inputs):
    import numpy as _np
    import concourse.bacc as _bacc
    from concourse import mybir as _mybir
    from concourse.bass_utils import run_bass_kernel_spmd as _run

    nc = _bacc.Bacc("TRN2", target_bir_lowering=False, num_devices=1)
    arrays, args = {}, []
    for name in _INS:
        a = _np.ascontiguousarray(inputs[name])
        arrays[f"in_{name}_dram"] = a
        args.append(nc.dram_tensor(f"in_{name}_dram", a.shape, _mybir.dt.from_np(a.dtype), kind="ExternalInput").ap())
    for i, (shape, dtype) in enumerate(_OUTS):
        dt = _mybir.dt.from_np(_np.dtype(dtype))
        args.append(nc.dram_tensor(f"out_{i}_dram", shape, dt, kind="ExternalOutput").ap())
    macaron_block(nc, *args)
    r = _run(nc, [arrays], core_ids=[0])
    got = tuple(r.results[0][f"out_{i}_dram"] for i in range(len(_OUTS)))
    return got[0]
```
